# Optimizing a Trainium2 kernel written in Bass

```python
import numpy as np
import jax
import jax.numpy as jnp

def _softmax(x, axis=-1):
    return jax.nn.softmax(x, axis=axis)

def _gelu(x):
    return jax.nn.gelu(x, approximate=True)

def _silu(x):
    return jax.nn.silu(x)

def _sigmoid(x):
    return jax.nn.sigmoid(x)

def _layernorm(x, axis=-1, eps=1e-05):
    m = jnp.mean(x, axis=axis, keepdims=True)
    v = jnp.var(x, axis=axis, keepdims=True)
    return (x - m) / jnp.sqrt(v + eps)

def _scatter_add(tgt, idx, src, axis=0):
    return tgt.at[idx].add(src)

def _segment_sum(src, seg, n):
    return jax.ops.segment_sum(src, seg, n)
kernel_name = 'mk_seq_preln_d1_jaxref_r4_7b5705'

def setup_inputs(seed: int=0):
    np.random.seed(seed)
    _w = jnp.asarray

    def _L0_attn_setup():
        import jax, jax.numpy as jnp
        import numpy as np
        D_MODEL = 512
        N_HEADS = 32
        N_KV_HEADS = 8
        D_K = D_MODEL // N_HEADS
        REPS = N_HEADS // N_KV_HEADS
        B, S = (2, 512)
        key = jax.random.key(seed)
        ks = jax.random.split(key, 6)
        sd = 1.0 / np.sqrt(D_MODEL)
        return {'x': jax.random.normal(ks[0], (B, S, D_MODEL), jnp.float32), 'Wq': jax.random.normal(ks[1], (D_MODEL, N_HEADS * D_K), jnp.float32) * sd, 'bq': jnp.zeros((N_HEADS * D_K,), jnp.float32), 'Wk': jax.random.normal(ks[2], (D_MODEL, N_KV_HEADS * D_K), jnp.float32) * sd, 'bk': jnp.zeros((N_KV_HEADS * D_K,), jnp.float32), 'Wv': jax.random.normal(ks[3], (D_MODEL, N_KV_HEADS * D_K), jnp.float32) * sd, 'bv': jnp.zeros((N_KV_HEADS * D_K,), jnp.float32), 'Wo': jax.random.normal(ks[4], (N_HEADS * D_K, D_MODEL), jnp.float32) * sd, 'bo': jnp.zeros((D_MODEL,), jnp.float32)}
    _L0_attn_in = _L0_attn_setup()

    def _L0_ffn_setup():
        import jax, jax.numpy as jnp
        import numpy as np
        NUM_EXPERTS_PER_TOK = 2
        key = jax.random.key(seed)
        k1, k2, k3, k4 = jax.random.split(key, 4)
        B, S, D, O, E = (4, 512, 512, 512, 8)
        x = jax.random.normal(k1, (B, S, D), dtype=jnp.float32)
        gate_w = jax.random.normal(k2, (E, D), dtype=jnp.float32) * (1.0 / np.sqrt(D))
        expert_w = jax.random.normal(k3, (E, O, D), dtype=jnp.float32) * (1.0 / np.sqrt(D))
        expert_b = jax.random.normal(k4, (E, O), dtype=jnp.float32) * 0.01
        return {'x': x, 'gate_w': gate_w, 'expert_w': expert_w, 'expert_b': expert_b}
    _L0_ffn_in = _L0_ffn_setup()
    _d = {'L0_attn_x': _L0_attn_in['x'], 'L0_attn_Wq': _L0_attn_in['Wq'], 'L0_attn_bq': _L0_attn_in['bq'], 'L0_attn_Wk': _L0_attn_in['Wk'], 'L0_attn_bk': _L0_attn_in['bk'], 'L0_attn_Wv': _L0_attn_in['Wv'], 'L0_attn_bv': _L0_attn_in['bv'], 'L0_attn_Wo': _L0_attn_in['Wo'], 'L0_attn_bo': _L0_attn_in['bo'], 'L0_ffn_gate_w': _L0_ffn_in['gate_w'], 'L0_ffn_expert_w': _L0_ffn_in['expert_w'], 'L0_ffn_expert_b': _L0_ffn_in['expert_b']}
    _x0 = _d['L0_attn_x']
    _d['L0_attn_x'] = jax.random.normal(jax.random.fold_in(jax.random.key(seed), 1), (1, 2048, 512), dtype=_x0.dtype)
    del _x0
    return _d

def reference(L0_attn_x, L0_attn_Wq, L0_attn_bq, L0_attn_Wk, L0_attn_bk, L0_attn_Wv, L0_attn_bv, L0_attn_Wo, L0_attn_bo, L0_ffn_gate_w, L0_ffn_expert_w, L0_ffn_expert_b):

    def _L0_attn_ref(x, Wq, bq, Wk, bk, Wv, bv, Wo, bo):
        import jax, jax.numpy as jnp
        import numpy as np
        D_MODEL = 512
        N_HEADS = 32
        N_KV_HEADS = 8
        D_K = D_MODEL // N_HEADS
        REPS = N_HEADS // N_KV_HEADS
        B, S = (2, 512)
        b, s, _ = x.shape
        Q = (x @ Wq + bq).reshape(b, s, N_HEADS, D_K).transpose(0, 2, 1, 3)
        K = (x @ Wk + bk).reshape(b, s, N_KV_HEADS, D_K).transpose(0, 2, 1, 3)
        V = (x @ Wv + bv).reshape(b, s, N_KV_HEADS, D_K).transpose(0, 2, 1, 3)
        K = jnp.repeat(K, REPS, axis=1)
        V = jnp.repeat(V, REPS, axis=1)
        scores = jnp.einsum('bhqd,bhkd->bhqk', Q, K) / jnp.sqrt(jnp.float32(D_K))
        attn = jax.nn.softmax(scores, axis=-1)
        out = jnp.einsum('bhqk,bhkd->bhqd', attn, V)
        out = out.transpose(0, 2, 1, 3).reshape(b, s, N_HEADS * D_K)
        return out @ Wo + bo

    def _L0_ffn_ref(x, gate_w, expert_w, expert_b):
        import jax, jax.numpy as jnp
        import numpy as np
        NUM_EXPERTS_PER_TOK = 2
        B, S, D = x.shape
        xf = x.reshape(B * S, D)
        gate_logits = xf @ gate_w.T
        top_vals, top_idx = jax.lax.top_k(gate_logits, NUM_EXPERTS_PER_TOK)
        w = jax.nn.softmax(top_vals.astype(jnp.float32), axis=-1).astype(x.dtype)
        y_all = jnp.einsum('td,eod->teo', xf, expert_w) + expert_b[None, :, :]
        y_sel = jnp.take_along_axis(y_all, top_idx[:, :, None], axis=1)
        out = jnp.sum(y_sel * w[:, :, None], axis=1)
        return out.reshape(B, S, -1)
    x = L0_attn_x
    x = x + _L0_attn_ref(_layernorm(x, axis=-1), L0_attn_Wq, L0_attn_bq, L0_attn_Wk, L0_attn_bk, L0_attn_Wv, L0_attn_bv, L0_attn_Wo, L0_attn_bo)
    x = x + _L0_ffn_ref(_layernorm(x, axis=-1), L0_ffn_gate_w, L0_ffn_expert_w, L0_ffn_expert_b)
    return x

_drawn_inputs = setup_inputs


def setup_inputs(seed=0):
    import zlib

    import numpy as np

    out = dict(_drawn_inputs(seed))
    spreads = {'L0_attn_bq': (0.0, 0.312),
     'L0_attn_bk': (0.0, 0.8),
     'L0_attn_bv': (0.0, 0.1),
     'L0_attn_bo': (0.0, 0.1)}
    factors = {'L0_ffn_expert_b': 8.0}
    for name, (base, spread) in spreads.items():
        noise = np.random.default_rng([zlib.crc32(name.encode()), seed]).standard_normal(out[name].shape)
        drawn = base * np.exp(spread * noise) if base else spread * noise
        out[name] = jnp.asarray(drawn.astype(out[name].dtype))
    for name, factor in factors.items():
        out[name] = (out[name] * factor).astype(out[name].dtype)
    return out
```

```python
from contextlib import ExitStack

import concourse.bass as bass
from concourse import mybir

ALU = mybir.AluOpType
ACT = mybir.ActivationFunctionType
AX = mybir.AxisListType
F32 = mybir.dt.float32
BF16 = mybir.dt.bfloat16
U32 = mybir.dt.uint32
F32R = mybir.dt.float32r

P = 128
EPS = 1e-5


def preln_attention_moe(nc, x, Wq, bq, Wk, bk, Wv, bv, Wo, bo, gate_w, expert_w, expert_b, out):
    _, T, D = x.shape
    E = gate_w.shape[1]
    KVD = Wk.shape[1]
    DK = 16
    G = KVD // DK
    REP = D // KVD
    KD = D // P
    CH = 512
    NC = T // CH
    TT = CH // P
    NKT = T // P
    NKC = T // CH
    N = G * NC
    SCALE = DK ** -0.5

    Q_PART = [0, 1, 2, 0, 1, 0]
    K_PART = [0, 0, 0, 1, 1, 2]
    NTERM = len(Q_PART)
    CROW = NTERM * DK
    SROW = CROW + 3

    SLOTS = 8
    LEAD = 2
    PRING = 16
    UNITS = NKT * REP
    MUNITS = REP * TT * NKC // 2

    q_parts = nc.dram_tensor("q_parts", [3, D, T], BF16).ap()
    k_parts = nc.dram_tensor("k_parts", [3, KVD, T], BF16).ap()
    heads_out = nc.dram_tensor("heads_out", [N + 1, P, TT * REP * DK], F32).ap()

    x_t = x.rearrange("a (n p) d -> p (a n) d", p=P)
    out_t = out.rearrange("a (n p) d -> p (a n) d", p=P)

    with ExitStack() as ctx:
        def sb(name, shape, dt=F32):
            return ctx.enter_context(nc.sbuf_tensor(name, shape, dt))

        def sem(name):
            return ctx.enter_context(nc.semaphore(name))

        bank = ctx.enter_context(nc.psum_tensor("bank", [P, 8, CH], F32))

        v_cur = sb("v_cur", [P, NKT, 2 * DK])
        wo_hi = sb("wo_hi", [P, KD, D], F32R)
        wg_sb = sb("wg_sb", [P, KD, E])
        wg_hi = sb("wg_hi", [P, KD, E], F32R)
        wg_lo = sb("wg_lo", [P, KD, E], F32R)
        be_sb = sb("be_sb", [P, D])
        ident = sb("ident", [P, P])
        bq_sb = sb("bq_sb", [P, KD])
        bk_sb = sb("bk_sb", [P, 1])
        bo_sb = sb("bo_sb", [P, D])
        stats = sb("stats", [P, TT, 6])
        mv = sb("mv", [P, TT, 2])
        std = sb("std", [P, TT])
        rstd = sb("rstd", [P, TT])
        mv2 = sb("mv2", [P, NKT, 2])
        std2 = sb("std2", [P, NKT])
        rstd2 = sb("rstd2", [P, NKT])
        eps_sb = sb("eps_sb", [P, 1])
        exp_warm = sb("exp_warm", [P, 1])
        max_kc = sb("max_kc", [P, MUNITS])
        max_q = sb("max_q", [P, REP * TT])
        negmax = sb("negmax", [REP * TT, P])
        shift = sb("shift", [REP * TT, 3, P], BF16)
        o_acc = sb("o_acc", [P, CH])
        o_rec = sb("o_rec", [P, TT, REP, 1])
        o_norm = sb("o_norm", [P, TT, REP, DK])
        iota_f = sb("iota_f", [P, E])
        xn2 = sb("xn2", [P, 2, D])
        logits = sb("logits", [P, 2, E])
        top = sb("top", [P, 2, 8])
        top_i = sb("top_i", [P, 2, 8], U32)
        top_f = sb("top_f", [P, 2, 2])
        g_exp = sb("g_exp", [P, 2, 3])
        g_w = sb("g_w", [P, 2, 2])
        g_tmp = sb("g_tmp", [P, 2, E])
        g_pad = sb("g_pad", [P, 2, P])
        g_padT = sb("g_padT", [P, 2, P])

        def in_turn(*turns):
            made = []
            for turn in turns:
                with ExitStack() as stack:
                    made.append([stack.enter_context(nc.sbuf_tensor(name, shape, dt)) for name, shape, dt in turn])
            return made

        with nc.sbuf_tensor("we_raw", [P, E, KD, D], F32) as we_raw:
            pass
        we_lo = sb("we_lo", [P, E, KD, D], F32R)
        with nc.sbuf_tensor("wo_raw", [P, KD, D], F32) as wo_raw:
            pass
        wo_lo = sb("wo_lo", [P, KD, D], F32R)

        (arena_q, arena_k, arena_p, v_all), = in_turn(
            [("arena_q", [P, 8192], F32),
             ("arena_k", [P, 8192], F32),
             ("arena_p", [P, 8192], F32),
             ("v_all", [P, NKT, KVD], F32)])
        x2_all = sb("x2_all", [P, NKT, D])
        EA = 6
        we_hi_a = sb("we_hi_a", [P, EA, KD, D], F32R)
        (atT_hi, atT_lo, at), (we_hi_b, x2T_hi, x2T_lo) = in_turn(
            [("atT_hi", [P, KD, CH], F32R), ("atT_lo", [P, KD, CH], F32R), ("at", [P, TT, D], F32)],
            [("we_hi_b", [P, E - EA, KD, D], F32R), ("x2T_hi", [P, 2, KD, P], F32R), ("x2T_lo", [P, 2, KD, P], F32R)])

        def we_hi(e):
            return we_hi_a[:, e, :, :] if e < EA else we_hi_b[:, e - EA, :, :]

        x_all = arena_q[:, 0:8192].rearrange("p (n d) -> p n d", d=D)
        qf = arena_k[:, 1792:4352].rearrange("p (u s) -> p u s", u=5)
        parts = arena_k[:, 4352:8192].bitcast(BF16).rearrange("p (u a s) -> p u a s", u=5, a=3)
        xn = arena_p[:, 0:2048].rearrange("p (n d) -> p n d", d=D)
        xT = arena_p[:, 2048:4096].rearrange("p (k s) -> p k s", k=KD)
        wq_sb = arena_p[:, 4096:6144].rearrange("p (k n) -> p k n", k=KD)
        wk_sb = arena_p[:, 6144:6656].rearrange("p (k n) -> p k n", k=KD)
        wv_sb = arena_p[:, 6656:7168].rearrange("p (k n) -> p k n", k=KD)
        bv_sb = arena_p[:, 7168:7680].rearrange("p (t n) -> p t n", t=TT)
        q_st = arena_q[:, :].bitcast(BF16).rearrange("p (c h s) -> p c h s", c=SLOTS, h=REP)
        q_flat = arena_q[:, :].bitcast(BF16)
        k_st = arena_k[:, :].bitcast(BF16).rearrange("p (g s) -> p g s", g=G)
        k_flat = arena_k[:, :].bitcast(BF16)
        probs = arena_p[:, :].rearrange("p (r s) -> p r s", r=PRING)
        x_dma = [sem(f"x_dma{c}") for c in range(NC)]
        x_ready = sem("x_ready")
        wa_dma = sem("wa_dma")
        wc_dma = sem("wc_dma")
        consts = sem("consts")
        ident_ready = sem("ident_ready")
        iota_ready = sem("iota_ready")
        pool_step = sem("pool_step")
        mv_ready = sem("mv_ready")
        std_ready = sem("std_ready")
        xn_ready = sem("xn_ready")
        t_full = sem("t_full")
        t_evac = sem("t_evac")
        proj_full = sem("proj_full")
        proj_evac = sem("proj_evac")
        v_full = sem("v_full")
        v_evac = sem("v_evac")
        hi_ready = sem("hi_ready")
        parts_ready = sem("parts_ready")
        parts_stored = sem("parts_stored")
        step_n = sem("step_n")
        step_s = sem("step_s")
        k0_dma = sem("k0_dma")
        kr_dma = sem("kr_dma")
        q_dma = sem("q_dma")
        s_full = sem("s_full")
        p_ready = sem("p_ready")
        pv_done = sem("pv_done")
        v_ready = sem("v_ready")
        m_full = sem("m_full")
        m_done = sem("m_done")
        maxq_ready = sem("maxq_ready")
        mT_full = sem("mT_full")
        neg_ready = sem("neg_ready")
        ones_ready = sem("ones_ready")
        step_m = sem("step_m")
        shift_ready = sem("shift_ready")
        shift_dma = sem("shift_dma")
        o_ready = sem("o_ready")
        oT_full = sem("oT_full")
        rec_ready = sem("rec_ready")
        onorm_ready = sem("onorm_ready")
        o_dma = sem("o_dma")
        at_dma = sem("at_dma")
        xr_dma = sem("xr_dma")
        xb_ready = sem("xb_ready")
        wo_split = sem("wo_split")
        we_split = sem("we_split")
        wlo_ready = sem("wlo_ready")
        elo_ready = sem("elo_ready")
        at_full = sem("at_full")
        at_hi = sem("at_hi")
        at_evac = sem("at_evac")
        wo_full = sem("wo_full")
        x2_ready = sem("x2_ready")
        step_c = sem("step_c")
        step_g = sem("step_g")
        mv2_ready = sem("mv2_ready")
        std2_ready = sem("std2_ready")
        xn2_ready = sem("xn2_ready")
        xt_full = sem("xt_full")
        xt_hi = sem("xt_hi")
        xt_evac = sem("xt_evac")
        gl_full = sem("gl_full")
        gl_evac = sem("gl_evac")
        gd_ready = sem("gd_ready")
        ge_ready = sem("ge_ready")
        gw_ready = sem("gw_ready")
        gT_full = sem("gT_full")
        gT_evac = sem("gT_evac")
        y_full = sem("y_full")
        y_done = sem("y_done")
        out_dma = sem("out_dma")

        sp_passed = sem("sp_passed")
        dve_passed = sem("dve_passed")

        YU = E + 1
        YR = 3

        block = ctx.enter_context(nc.Block())

        @block.gpsimd
        def _(pool):
            pool.memset(ident[:, :], 0.0).then_inc(pool_step, 1)
            pool.wait_ge(pool_step, 1)
            pool.affine_select(out=ident[:, :], in_=ident[:, :], compare_op=ALU.not_equal, fill=1.0,
                               base=0, pattern=[[-1, P]], channel_multiplier=1).then_inc(ident_ready, 1)
            pool.iota(iota_f[:, :], [[1, E]], base=0, channel_multiplier=0,
                      allow_small_or_imprecise_dtypes=True).then_inc(iota_ready, 1)
            pool.dma_start(wo_raw[:, :, :], Wo.rearrange("(k p) n -> p k n", p=P)).then_inc(wc_dma, 16)
            pool.dma_start(wg_sb[:, :, :], gate_w.rearrange("(k p) n -> p k n", p=P)).then_inc(wc_dma, 16)
            pool.wait_ge(consts, 5)
            pool.dma_start(be_sb[0:E, :], expert_b).then_inc(wc_dma, 16)
            pool.dma_start(bo_sb[:, :], bo.partition_broadcast(P)).then_inc(wc_dma, 16)
            for e in range(E):
                pool.dma_start(we_raw[:, e, :, :],
                               expert_w[e].rearrange("(k p) n -> p k n", p=P)).then_inc(wc_dma, 16)

            pool.wait_ge(ident_ready, 1)
            pool.wait_ge(iota_ready, 1)
            pool.memset(k_st[CROW:SROW, 0, :], 1.0).then_inc(ones_ready, 1)
            pool.wait_ge(parts_stored, 1 + 16 * 5 * NC)
            pool.wait_ge(ones_ready, 1)
            pool.memset(k_st[CROW:SROW, 1:G, :], 1.0).then_inc(ones_ready, 1)

            pool.wait_ge(ones_ready, 2)
            pool.wait_ge(v_evac, 1 + NC)
            with pool.Fori(0, G) as g:
                pool.wait_ge(pv_done, PRING // REP + NKT * NC * g)
                pool.tensor_copy(v_cur[:, :, 0:DK], v_all[:, :, bass.ds(g * DK, DK)]).then_inc(v_ready, 1)

            pool.wait_ge(wc_dma, 16 * (4 + E))
            pool.wait_ge(s_full, UNITS * N)
            for c in range(NC):
                pool.dma_start(x2_all[:, c * TT:(c + 1) * TT, :], x_t[:, c * TT:(c + 1) * TT, :]).then_inc(xr_dma, 16)
                pool.wait_ge(xr_dma, 16 * (c + 1))
                for t in range(TT):
                    tile = x2_all[:, c * TT + t, :]
                    pool.tensor_tensor(tile, tile, bo_sb[:, :], ALU.add).then_inc(xb_ready, 1)

        @block.sync
        def _(sp):
            for c in range(NC):
                sp.dma_start(x_all[:, c * TT:(c + 1) * TT, :], x_t[:, c * TT:(c + 1) * TT, :]).then_inc(x_dma[c], 16)
            for c in range(NC):
                sp.wait_ge(x_dma[c], 16)
                sp.sem_inc(x_ready, 1)

            def wait_first(s, value):
                sp.wait_ge(s, value)
                sp.sem_inc(sp_passed, 1)

            def store_parts(c, u):
                wait_first(parts_ready, 5 * c + u + 1)
                dst = k_parts if u == 0 else q_parts[:, (u - 1) * P:u * P, :]
                sp.dma_start(dst[:, :, bass.ds(c * CH, CH)].rearrange("a p s -> p a s"),
                             parts[:, u, :, :]).then_inc(parts_stored, 16)

            with sp.Fori(0, NC - 1) as c:
                for u in range(5):
                    store_parts(c, u)

            def load_keys(groups, done):
                for t in range(NTERM):
                    src = k_parts[K_PART[t]].rearrange("(g d) s -> d g s", d=DK)
                    sp.dma_start(k_st[t * DK:(t + 1) * DK, groups, :], src[:, groups, :]).then_inc(done, 16)

            def load_queries(j):
                g, qc, slot = j // NC, j % NC, j % SLOTS
                for t in range(NTERM):
                    src = q_parts[Q_PART[t]].rearrange("(f d) s -> d f s", d=DK)
                    sp.dma_start(q_st[t * DK:(t + 1) * DK, bass.ds(slot, 1), :, :].squeeze(1),
                                 src[:, bass.ds(g * REP, REP), bass.ds(qc * CH, CH)]).then_inc(q_dma, 16)
                wait_first(q_dma, 16 * NTERM * (j + 1))

            def place_shift(j):
                wait_first(shift_ready, j + 1)
                for a in range(3):
                    dst = q_st[CROW + a:CROW + a + 1, bass.ds(j % SLOTS, 1), :, :].squeeze(1)
                    sp.dma_start(dst.rearrange("o h (t q) -> o (h t) q", t=TT),
                                 shift[:, a, :]).then_inc(shift_dma, 16)
                wait_first(shift_dma, 1 + 48 * (j + 1))

            def store_heads(i):
                wait_first(onorm_ready, 1 + i + 1)
                sp.dma_start(heads_out[bass.ds(i, 1)].squeeze(0),
                             o_norm[:, :, :, :].rearrange("p t h d -> p (t h d)")).then_inc(o_dma, 16)

            store_parts(NC - 1, 0)
            sp.wait_ge(parts_stored, 1 + 16 * (5 * (NC - 1) + 1))
            load_keys(slice(0, 1), k0_dma)
            for j in range(LEAD):
                load_queries(j)
            for u in range(1, 5):
                store_parts(NC - 1, u)
            sp.wait_ge(parts_stored, 1 + 16 * 5 * NC)
            load_keys(slice(1, G), kr_dma)
            with sp.Fori(LEAD, SLOTS) as j:
                load_queries(j)
            place_shift(0)
            with sp.Fori(0, N - SLOTS) as i:
                store_heads(i)
                place_shift(i + 1)
                wait_first(s_full, UNITS * (i + 1))
                load_queries(i + SLOTS)
            with sp.Fori(N - SLOTS, N - 2) as i:
                store_heads(i)
                place_shift(i + 1)

            def load_heads(c):
                for g in range(G):
                    sp.dma_start(at[:, :, g * REP * DK:(g + 1) * REP * DK],
                                 heads_out[bass.ds(c + (g * NC + 1), 1)].squeeze(0).rearrange(
                                     "p (t f) -> p t f", t=TT)).then_inc(at_dma, 16)

            sp.wait_ge(o_dma, 1 + 16 * (N - 2))
            sp.wait_ge(v_ready, G)
            load_heads(0)
            store_heads(N - 2)
            place_shift(N - 1)
            for i in (N - 1, N):
                store_heads(i)

            sp.wait_ge(o_dma, 1 + 16 * (N + 1))
            with sp.Fori(1, NC) as c:
                wait_first(at_full, TT * c)
                load_heads(c)
            with sp.Fori(0, NKT) as n:
                wait_first(y_done, YR + YU * (n + 1))
                sp.dma_start(out_t[:, bass.ds(n, 1), :], x2_all[:, bass.ds(n, 1), :]).then_inc(out_dma, 16)
            sp.wait_ge(out_dma, 16 * NKT)

        @block.scalar
        def _(act):
            for s, n in ((t_evac, 2), (proj_evac, 5), (p_ready, 2)):
                act.sem_inc(s, n)
            act.dma_start(wk_sb[:, :, :], Wk.rearrange("(k p) n -> p k n", p=P)).then_inc(wa_dma, 16)
            act.dma_start(wq_sb[:, :, :], Wq.rearrange("(k p) n -> p k n", p=P)).then_inc(wa_dma, 16)
            act.dma_start(wv_sb[:, :, :], Wv.rearrange("(k p) n -> p k n", p=P)).then_inc(wa_dma, 16)
            act.dma_start(bq_sb[:, :], bq).then_inc(wa_dma, 16)
            act.dma_start(bk_sb[:, :], bk).then_inc(wa_dma, 16)
            for t in range(TT):
                act.dma_start(bv_sb[:, t, :], bv.partition_broadcast(P)).then_inc(wa_dma, 16)
            act.wait_ge(consts, 1)

            def evacuate_transposes(n, dst, t):
                act.wait_ge(t_full, n + 1)
                act.activation(dst[:, :, t * P:(t + 1) * P],
                               bank[:, 6 + t % 2, :].rearrange("p (k s) -> p k s", k=KD),
                               ACT.Copy).then_inc(t_evac, 1)

            def deviation(c):
                act.wait_ge(mv_ready, c + 1)
                act.activation(std[:, :], mv[:, :, 1], ACT.Sqrt, bias=eps_sb[:, 0:1]).then_inc(std_ready, 1)

            def project_chunk(c, last):
                for t in range(TT):
                    evacuate_transposes(c * TT + t, xT, t)
                if not last:
                    deviation(c + 1)
                act.wait_ge(parts_stored, 1 + 16 * 5 * c)
                for u in range(5):
                    act.wait_ge(proj_full, 5 * c + u + 1)
                    bias = bk_sb[:, 0:1] if u == 0 else bq_sb[:, u - 1:u]
                    act.activation(qf[:, u, :], bank[:, u, :], ACT.Identity, bias=bias).then_inc(proj_evac, 1)
                    act.wait_ge(proj_evac, 5 + 5 * c + u + 1)
                    act.activation(parts[:, u, 0, :], qf[:, u, :], ACT.Copy).then_inc(hi_ready, 1)

            deviation(0)
            act.wait_ge(wa_dma, 16 * 9)
            with act.Fori(0, NC - 1) as c:
                project_chunk(c, False)
            project_chunk(NC - 1, True)

            act.wait_ge(wc_dma, 16 * (4 + E))
            act.activation(wo_hi[:, :, :], wo_raw[:, :, :], ACT.Copy).then_inc(wo_split, 1)
            act.activation(wg_hi[:, :, :], wg_sb[:, :, :], ACT.Copy).then_inc(wo_split, 1)

            act.activation(exp_warm[:, :], eps_sb[:, :], ACT.Exp)
            with act.Fori(0, N) as i:
                for u in range(UNITS):
                    act.wait_ge(s_full, UNITS * i + u + 1)
                    if u % REP == 0:
                        act.wait_ge(pv_done, NKT * i + u // REP + 1)
                    act.activation(probs[:, u % PRING, :], bank[:, u % 2, :],
                                   ACT.Exp, scale=SCALE).then_inc(p_ready, 1)

            def hi(dst, src):
                return act.activation(dst, src, ACT.Copy)

            def expert_hi(e, dst):
                hi(dst, we_raw[:, bass.ds(e, 1), :, :].squeeze(1)).then_inc(we_split, 1)

            def attention_hi(c):
                for t in range(TT):
                    act.wait_ge(at_full, TT * c + t + 1)
                    hi(atT_hi[:, :, t * P:(t + 1) * P],
                       bank[:, 2 + t % 2, :].rearrange("p (k s) -> p k s", k=KD)).then_inc(at_hi, 1)

            act.wait_ge(pv_done, PRING // REP + NKT * N)
            with act.Fori(0, NC - 1) as c:
                attention_hi(c)
                for q in range(2):
                    expert_hi(2 * c + q, we_hi_a[:, bass.ds(2 * c + q, 1), :, :].squeeze(1))
            attention_hi(NC - 1)
            act.wait_ge(mv2_ready, NC)
            act.activation(std2[:, :], mv2[:, :, 1], ACT.Sqrt, bias=eps_sb[:, 0:1]).then_inc(std2_ready, 1)
            act.wait_ge(wo_full, NKT)
            for e in range(EA, E):
                hi(we_hi(e), we_raw[:, e, :, :]).then_inc(we_split, 1)

            def gate_tile(n, b):
                act.wait_ge(xt_full, n + 1)
                hi(x2T_hi[:, b, :, :], bank[:, 6, :].rearrange("p (k s) -> p k s", k=KD)).then_inc(xt_hi, 1)
                act.wait_ge(gd_ready, n + 1)
                act.activation(g_exp[:, b, 1:2], g_exp[:, b, 0:1], ACT.Exp).then_inc(ge_ready, 1)
                act.wait_ge(gT_full, n + 1)
                act.activation(g_padT[:, b, :], bank[:, 7, P:2 * P], ACT.Copy).then_inc(gT_evac, 1)

            with act.Fori(0, NKT // 2) as m:
                for b in range(2):
                    gate_tile(2 * m + b, b)

        @block.tensor
        def _(pe):
            pe.wait_ge(ident_ready, 1)
            pe.wait_ge(consts, 5)

            def transpose_tile(n, src, ready, t):
                pe.wait_ge(ready, n[0])
                pe.wait_ge(t_evac, n[1])
                for k in range(KD):
                    mm = pe.transpose(bank[:, 6 + t % 2, k * P:(k + 1) * P], src[:, t, k * P:(k + 1) * P], ident[:, :])
                mm.then_inc(t_full, 1)

            with pe.Fori(0, NC) as c:
                for t in range(TT):
                    transpose_tile((c * TT + t + 1, c * TT + t + 1), xn, xn_ready, t)
                pe.wait_ge(wa_dma, 16 * 9)
                pe.wait_ge(t_evac, 2 + TT * (c + 1))
                for u in range(5):
                    pe.wait_ge(proj_evac, 5 * c + u + 1)
                    for k in range(KD):
                        w = wk_sb[:, k, :] if u == 0 else wq_sb[:, k, (u - 1) * P:u * P]
                        mm = pe.matmul(bank[:, u, :], w, xT[:, k, :], start=(k == 0), stop=(k == KD - 1))
                    mm.then_inc(proj_full, 1)
                pe.wait_ge(v_evac, c + 1)
                for t in range(TT):
                    for k in range(KD):
                        mm = pe.matmul(bank[:, 5, t * KVD:(t + 1) * KVD], xT[:, k, t * P:(t + 1) * P],
                                       wv_sb[:, k, :], start=(k == 0), stop=(k == KD - 1))
                mm.then_inc(v_full, 1)

            def max_unit(j, m):
                h, qt, half = m // (2 * TT), m // 2 % TT, m % 2
                pe.wait_ge(m_done, MUNITS * j + m + 1)
                qo = (j % SLOTS) * (REP * CH) + h * CH + qt * P
                for q in range(2):
                    mm = pe.matmul(bank[:, 2 + 2 * (m % 2) + q, :], q_flat[0:CROW, bass.ds(qo, P)],
                                   k_flat[0:CROW, bass.ds((j // NC) * T + (2 * half + q) * CH, CH)],
                                   start=True, stop=True)
                mm.then_inc(m_full, 1)

            def max_transpose(j):
                pe.wait_ge(maxq_ready, j + 1)
                pe.transpose(bank[0:REP * TT, 7, 0:P], max_q[:, :], ident[:, :]).then_inc(mT_full, 1)

            def score_unit(i, u):
                kt, h = u // REP, u % REP
                pe.wait_ge(p_ready, UNITS * i + u + 1)
                qo = (i % SLOTS) * (REP * CH) + h * CH
                pe.matmul(bank[:, u % 2, :], k_flat[0:SROW, bass.ds((i // NC) * T + kt * P, P)],
                          q_flat[0:SROW, bass.ds(qo, CH)], start=True, stop=True).then_inc(s_full, 1)

            def value_product(i, kt):
                pe.wait_ge(p_ready, 2 + UNITS * i + REP * (kt + 1))
                for h in range(REP):
                    mm = pe.matmul(bank[32 * h:32 * h + 32, 6, :], v_cur[:, kt, :],
                                   probs[:, (REP * kt + h) % PRING, :],
                                   start=(kt == 0), stop=(kt == NKT - 1))
                mm.then_inc(pv_done, 1)

            def output_transpose(i):
                pe.wait_ge(o_ready, i + 1)
                pe.wait_ge(neg_ready, min(i, N - 1) + 2 if isinstance(i, int) else i + 2)
                for t in range(TT):
                    mm = pe.transpose(bank[:, 7, t * P:(t + 1) * P], o_acc[:, t * P:(t + 1) * P], ident[:, :])
                mm.then_inc(oT_full, 1)

            pe.wait_ge(proj_evac, 5 + 5 * NC)
            pe.wait_ge(v_evac, 1 + NC)
            pe.wait_ge(t_evac, 2 + NKT)
            pe.wait_ge(k0_dma, 16 * NTERM)
            for j in range(LEAD):
                pe.wait_ge(q_dma, 16 * NTERM * (j + 1))
                for m in range(MUNITS):
                    max_unit(j, m)
                if j < LEAD - 1:
                    max_transpose(j)
            pe.wait_ge(kr_dma, 16 * NTERM)
            pe.wait_ge(ones_ready, 2)

            def round_(i, with_max, with_shift):
                pe.wait_ge(shift_dma, 1 + 48 * (i + 1))
                if with_max:
                    pe.wait_ge(q_dma, 16 * NTERM * (i + LEAD + 1))
                pe.wait_ge(v_ready, i // NC + 1)
                for kt in range(NKT):
                    score_unit(i, REP * kt)
                    score_unit(i, REP * kt + 1)
                    if with_max:
                        max_unit(i + LEAD, 2 * kt)
                    if with_max and kt < NKT - 1:
                        max_unit(i + LEAD, 2 * kt + 1)
                    score_unit(i, REP * kt + 2)
                    score_unit(i, REP * kt + 3)
                    if with_max and kt == NKT - 1:
                        max_unit(i + LEAD, 2 * kt + 1)
                    if kt >= 1:
                        if kt == 1:
                            pe.wait_ge(o_ready, i + 1)
                        value_product(i, kt - 1)
                    if kt == 2:
                        output_transpose(i)
                    if kt == 5 and with_shift:
                        pe.wait_ge(onorm_ready, i + 2)
                        max_transpose(i + 1)
                value_product(i, NKT - 1)

            with pe.Fori(0, N - LEAD) as i:
                round_(i, True, True)
            round_(N - 2, False, True)
            round_(N - 1, False, False)
            output_transpose(N)

            def product(out_, lhs, rhs, first=True, last=True):
                terms = [(lhs[0], rhs[0]), (lhs[1], rhs[0]), (lhs[0], rhs[1])]
                for q, (a, w) in enumerate(terms):
                    for k in range(KD):
                        mm = pe.matmul(out_, a(k), w(k), start=(q == 0 and k == 0), stop=(q == 2 and k == KD - 1))
                return mm

            pe.wait_ge(m_done, 2 + MUNITS * N)
            pe.wait_ge(o_ready, 1 + N)
            pe.wait_ge(p_ready, 2 + UNITS * N)
            pe.wait_ge(wlo_ready, 2)
            with pe.Fori(0, NC) as c:
                pe.wait_ge(at_dma, 16 * G * (c + 1))
                for t in range(TT):
                    pe.wait_ge(at_evac, TT * c + t + 1)
                    for k in range(KD):
                        mm = pe.transpose(bank[:, 2 + t % 2, k * P:(k + 1) * P], at[:, t, k * P:(k + 1) * P], ident[:, :])
                    mm.then_inc(at_full, 1)
                for t in range(TT):
                    pe.wait_ge(at_evac, 2 + TT * c + t + 1)
                    pe.wait_ge(x2_ready, TT * c + t + 1)
                    product(bank[:, 4 + t % 2, :],
                            [lambda k: atT_hi[:, k, t * P:(t + 1) * P], lambda k: atT_lo[:, k, t * P:(t + 1) * P]],
                            [lambda k: wo_hi[:, k, :], lambda k: wo_lo[:, k, :]]).then_inc(wo_full, 1)

            def transpose_x(n, b):
                pe.wait_ge(xn2_ready, n + 1)
                for k in range(KD):
                    mm = pe.transpose(bank[:, 6, k * P:(k + 1) * P], xn2[:, b, k * P:(k + 1) * P], ident[:, :])
                mm.then_inc(xt_full, 1)

            def halves(b):
                return [lambda k: x2T_hi[:, b, k, :], lambda k: x2T_lo[:, b, k, :]]

            def gate_logits(n, b):
                pe.wait_ge(xt_evac, n + 1)
                product(bank[:, 7, 0:E], halves(b),
                        [lambda k: wg_hi[:, k, :], lambda k: wg_lo[:, k, :]]).then_inc(gl_full, 1)

            def transpose_gate(n, b):
                pe.wait_ge(gw_ready, n + 1)
                pe.transpose(bank[:, 7, P:2 * P], g_pad[:, b, :], ident[:, :]).then_inc(gT_full, 1)

            def expert(n, b, e):
                pe.wait_ge(y_done, YU * n + e + 1)
                product(bank[:, e % YR, :], halves(b),
                        [lambda k: we_hi(e)[:, k, :], lambda k: we_lo[:, e, k, :]]).then_inc(y_full, 1)

            def expert_tile(n, b, first, last):
                nb = 1 - b
                for e in range(E):
                    if e == 1 and first:
                        transpose_gate(0, 0)
                    if e == (2 if first else 0) and not last:
                        transpose_x(n + 1, nb)
                    if e == 4 and not last:
                        gate_logits(n + 1, nb)
                    if e == 6 and not last:
                        transpose_gate(n + 1, nb)
                    if first:
                        pe.wait_ge(elo_ready, e + 1)
                    expert(n, b, e)
                pe.wait_ge(gT_evac, n + 1)
                pe.wait_ge(y_done, YU * n + E + 1)
                pe.matmul(bank[:, E % YR, :], g_padT[:, b, :], be_sb[:, :], start=True, stop=True).then_inc(y_full, 1)

            pe.wait_ge(onorm_ready, N + 2)
            transpose_x(0, 0)
            gate_logits(0, 0)
            expert_tile(0, 0, True, False)
            expert_tile(1, 1, False, False)
            with pe.Fori(1, NKT // 2 - 1) as m:
                for b in range(2):
                    expert_tile(2 * m + b, b, False, False)
            expert_tile(NKT - 2, 0, False, False)
            expert_tile(NKT - 1, 1, False, True)

        @block.vector
        def _(dve):
            for s, n in ((v_evac, 1), (parts_stored, 1), (pv_done, PRING // REP), (m_done, 2), (neg_ready, 1),
                         (shift_dma, 1), (o_ready, 1), (onorm_ready, 1), (o_dma, 1), (x2_ready, 2),
                         (at_evac, 2), (y_done, YR)):
                dve.sem_inc(s, n)
            dve.memset(eps_sb[:, :], EPS).then_inc(consts, 1)
            dve.memset(o_acc[:, :], 1.0).then_inc(consts, 1)
            dve.memset(v_cur[:, :, DK:2 * DK], 1.0).then_inc(consts, 1)
            dve.memset(g_pad[:, :, :], 0.0).then_inc(consts, 1)
            dve.memset(be_sb[:, :], 0.0).then_inc(consts, 1)

            def chain(s, base):
                n = [0]

                def link(ins):
                    n[0] += 1
                    ins.then_inc(s, 1)
                    dve.wait_ge(s, base + n[0])
                    dve.sem_inc(dve_passed, 1)
                return link

            STEPS_N, STEPS_S = TT * 2 + 1, 5 * 2

            def normalise_chunk(c):
                link = chain(step_n, STEPS_N * c)
                dve.wait_ge(x_ready, c + 1)
                for t in range(TT):
                    link(dve.bn_stats(stats[:, t, :], x_all[:, bass.ds(c * TT + t, 1), :].squeeze(1)))
                for t in range(TT):
                    link(dve.bn_aggr(mv[:, t, :], stats[:, t, :]))
                dve.sem_inc(mv_ready, 1)
                dve.wait_ge(std_ready, c + 1)
                link(dve.reciprocal(rstd[:, :], std[:, :]))
                if not isinstance(c, int):
                    dve.wait_ge(t_full, TT * c)
                for t in range(TT):
                    dve.tensor_scalar(xn[:, t, :], x_all[:, bass.ds(c * TT + t, 1), :].squeeze(1), mv[:, t, 0:1],
                                      rstd[:, t:t + 1], ALU.subtract, ALU.mult).then_inc(xn_ready, 1)

            def split_chunk(c):
                link = chain(step_s, STEPS_S * c)
                for u in range(5):
                    dve.wait_ge(hi_ready, 5 * c + u + 1)
                    link(dve.tensor_tensor(qf[:, u, :], qf[:, u, :], parts[:, u, 0, :], ALU.subtract))
                    link(dve.tensor_copy(parts[:, u, 1, :], qf[:, u, :]))
                    dve.tensor_tensor(parts[:, u, 2, :], qf[:, u, :], parts[:, u, 1, :],
                                      ALU.subtract).then_inc(parts_ready, 1)
                dve.wait_ge(v_full, c + 1)
                dve.tensor_tensor(v_all[:, bass.ds(c * TT, TT), :], bank[:, 5, :].rearrange("p (t n) -> p t n", t=TT),
                                  bv_sb[:, :, :], ALU.add).then_inc(v_evac, 1)

            normalise_chunk(0)
            with dve.Fori(0, NC - 1) as c:
                normalise_chunk(c + 1)
                split_chunk(c)
            split_chunk(NC - 1)

            dve.wait_ge(wo_split, 2)
            dve.tensor_tensor(wo_lo[:, :, :], wo_raw[:, :, :], wo_hi[:, :, :], ALU.subtract).then_inc(wlo_ready, 1)
            dve.tensor_tensor(wg_lo[:, :, :], wg_sb[:, :, :], wg_hi[:, :, :], ALU.subtract).then_inc(wlo_ready, 1)
            dve.wait_ge(iota_ready, 1)

            def reduce_unit(j, m):
                dve.wait_ge(m_full, MUNITS * j + m + 1)
                dve.reduce_max(max_kc[:, m:m + 1], bank[:, 2 + 2 * (m % 2):4 + 2 * (m % 2), :].rearrange("p a s -> p (a s)"),
                               AX.X).then_inc(m_done, 1)

            def combine_max(j):
                dve.wait_ge(m_done, 2 + MUNITS * (j + 1))
                dve.reduce_max(max_q[:, :], max_kc[:, :].rearrange("p (r c) -> p r c", c=2),
                               AX.X).then_inc(maxq_ready, 1)

            def make_shift(j):
                link = chain(step_m, 3 * j)
                dve.wait_ge(mT_full, j + 1)
                dve.wait_ge(shift_dma, 1 + 48 * j)
                dve.tensor_scalar(negmax[:, :], bank[0:REP * TT, 7, 0:P], -1.0, None, ALU.mult).then_inc(neg_ready, 1)
                dve.wait_ge(neg_ready, 1 + j + 1)
                link(dve.tensor_copy(shift[:, 0, :], negmax[:, :]))
                link(dve.tensor_tensor(negmax[:, :], negmax[:, :], shift[:, 0, :], ALU.subtract))
                link(dve.tensor_copy(shift[:, 1, :], negmax[:, :]))
                dve.tensor_tensor(shift[:, 2, :], negmax[:, :], shift[:, 1, :], ALU.subtract).then_inc(shift_ready, 1)

            def normalise(i):
                dve.wait_ge(oT_full, i + 1)
                dve.wait_ge(o_dma, 1 + 16 * i)
                o = bank[:, 7, :].rearrange("p (t h f) -> p t h f", t=TT, h=REP)
                dve.reciprocal(o_rec[:, :, :, :], o[:, :, :, DK:DK + 1]).then_inc(rec_ready, 1)
                dve.wait_ge(rec_ready, i + 1)
                dve.tensor_tensor(o_norm[:, :, :, :], o[:, :, :, 0:DK], o_rec[:, :, :, :].to_broadcast([P, TT, REP, DK]),
                                  ALU.mult).then_inc(onorm_ready, 1)

            for j in range(LEAD):
                for m in range(MUNITS):
                    reduce_unit(j, m)
                combine_max(j)
                dve.wait_ge(maxq_ready, j + 1)
                if j < LEAD - 1:
                    make_shift(j)

            def round_(i, with_max, with_shift):
                for kt in range(NKT):
                    if with_max:
                        for half in range(2):
                            reduce_unit(i + LEAD, 2 * kt + half)
                    if kt == 2:
                        normalise(i)
                    if kt == 5 and with_shift:
                        make_shift(i + 1)
                if with_max:
                    combine_max(i + LEAD)
                dve.wait_ge(pv_done, PRING // REP + NKT * (i + 1))
                dve.tensor_copy(o_acc[:, :], bank[:, 6, :]).then_inc(o_ready, 1)
                if with_max:
                    dve.wait_ge(maxq_ready, i + LEAD + 1)

            with dve.Fori(0, N - LEAD) as i:
                round_(i, True, True)
            round_(N - 2, False, True)
            round_(N - 1, False, False)
            normalise(N)

            def expert_lo(e, e_hi):
                dve.wait_ge(we_split, e + 1)
                dve.tensor_tensor(we_lo[:, bass.ds(e, 1), :, :].squeeze(1), we_raw[:, bass.ds(e, 1), :, :].squeeze(1), e_hi,
                                  ALU.subtract).then_inc(elo_ready, 1)

            STEPS_C = TT * 2 + 1
            with dve.Fori(0, NC) as c:
                link = chain(step_c, STEPS_C * c)
                for t in range(TT):
                    dve.wait_ge(at_hi, TT * c + t + 1)
                    dst = atT_lo[:, :, t * P:(t + 1) * P]
                    dve.tensor_tensor(dst, bank[:, 2 + t % 2, :].rearrange("p (k s) -> p k s", k=KD),
                                      atT_hi[:, :, t * P:(t + 1) * P], ALU.subtract).then_inc(at_evac, 1)
                for t in range(TT):
                    tile = x2_all[:, bass.ds(c * TT + t, 1), :].squeeze(1)
                    dve.wait_ge(wo_full, TT * c + t + 1)
                    dve.wait_ge(xb_ready, TT * c + t + 1)
                    dve.tensor_tensor(tile, bank[:, 4 + t % 2, :], tile, ALU.add).then_inc(x2_ready, 1)
                    dve.wait_ge(x2_ready, 2 + TT * c + t + 1)
                    dve.sem_inc(dve_passed, 1)
                    link(dve.bn_stats(stats[:, t, :], tile))
                    link(dve.bn_aggr(mv[:, t, :], stats[:, t, :]))
                link(dve.tensor_copy(mv2[:, bass.ds(c * TT, TT), :], mv[:, :, :]))
                dve.sem_inc(mv2_ready, 1)
                expert_lo(c, we_hi_a[:, bass.ds(c, 1), :, :].squeeze(1))
            dve.wait_ge(std2_ready, 1)
            dve.reciprocal(rstd2[:, :], std2[:, :]).then_inc(step_c, 1)
            dve.wait_ge(step_c, STEPS_C * NC + 1)

            def normalise_tile(n, b):
                dve.tensor_scalar(xn2[:, b, :], x2_all[:, bass.ds(n, 1), :].squeeze(1),
                                  mv2[:, bass.ds(n, 1), 0], rstd2[:, bass.ds(n, 1)],
                                  ALU.subtract, ALU.mult).then_inc(xn2_ready, 1)
                dve.wait_ge(xt_hi, n + 1)
                dve.tensor_tensor(x2T_lo[:, b, :, :], bank[:, 6, :].rearrange("p (k s) -> p k s", k=KD),
                                  x2T_hi[:, b, :, :], ALU.subtract).then_inc(xt_evac, 1)

            STEPS_G = 8

            def gate_top2(n, b):
                link = chain(step_g, STEPS_G * n)
                dve.wait_ge(gl_full, n + 1)
                link(dve.tensor_copy(logits[:, b, :], bank[:, 7, 0:E]))
                link(dve.max(top[:, b, :], logits[:, b, :]))
                link(dve.max_index(top_i[:, b, :], top[:, b, :], logits[:, b, :]))
                dve.tensor_tensor(g_exp[:, b, 0:1], top[:, b, 1:2], top[:, b, 0:1], ALU.subtract).then_inc(gd_ready, 1)
                link(dve.tensor_copy(top_f[:, b, :], top_i[:, b, 0:2]))
                return link

            def gate_weights(n, b, link):
                dve.wait_ge(ge_ready, n + 1)
                link(dve.tensor_scalar(g_exp[:, b, 2:3], g_exp[:, b, 1:2], 1.0, None, ALU.add))
                link(dve.reciprocal(g_w[:, b, 0:1], g_exp[:, b, 2:3]))
                link(dve.tensor_tensor(g_w[:, b, 1:2], g_exp[:, b, 1:2], g_w[:, b, 0:1], ALU.mult))
                dve.tensor_scalar(g_tmp[:, b, :], iota_f[:, :], top_f[:, b, 1:2], g_w[:, b, 1:2],
                                  ALU.is_equal, ALU.mult)
                link(dve.tensor_scalar(g_pad[:, b, 0:E], iota_f[:, :], top_f[:, b, 0:1], g_w[:, b, 0:1],
                                       ALU.is_equal, ALU.mult))
                dve.tensor_tensor(g_pad[:, b, 0:E], g_pad[:, b, 0:E], g_tmp[:, b, :], ALU.add).then_inc(gw_ready, 1)

            def add_expert(n, b, e):
                tile = x2_all[:, bass.ds(n, 1), :].squeeze(1)
                dve.wait_ge(y_full, YU * n + e + 1)
                dve.wait_ge(y_done, YR + YU * n + e)
                dve.scalar_tensor_tensor(tile, bank[:, e % YR, :], g_pad[:, b, e:e + 1], tile,
                                         ALU.mult, ALU.add).then_inc(y_done, 1)

            def expert_tile(n, b, first, last):
                nb = 1 - b
                dve.wait_ge(gw_ready, n + 1)
                if not last:
                    normalise_tile(n + 1, nb)
                for e in range(E):
                    if first and e < E - 4:
                        expert_lo(e + 4, we_hi(e + 4))
                    add_expert(n, b, e)
                    if e == 3 and not last:
                        link = gate_top2(n + 1, nb)
                    if e == 4 and not last:
                        gate_weights(n + 1, nb, link)
                tile = x2_all[:, bass.ds(n, 1), :].squeeze(1)
                dve.wait_ge(y_full, YU * n + E + 1)
                dve.wait_ge(y_done, YR + YU * n + E)
                dve.tensor_tensor(tile, bank[:, E % YR, :], tile, ALU.add).then_inc(y_done, 1)

            normalise_tile(0, 0)
            gate_weights(0, 0, gate_top2(0, 0))
            expert_tile(0, 0, True, False)
            expert_tile(1, 1, False, False)
            with dve.Fori(1, NKT // 2 - 1) as m:
                for b in range(2):
                    expert_tile(2 * m + b, b, False, False)
            expert_tile(NKT - 2, 0, False, False)
            expert_tile(NKT - 1, 1, False, True)


_INS = ["L0_attn_x", "L0_attn_Wq", "L0_attn_bq", "L0_attn_Wk", "L0_attn_bk", "L0_attn_Wv", "L0_attn_bv",
        "L0_attn_Wo", "L0_attn_bo", "L0_ffn_gate_w", "L0_ffn_expert_w", "L0_ffn_expert_b"]


def kernel(**inputs):
    import numpy as np
    import concourse.bacc as bacc
    from concourse.bass_utils import run_bass_kernel_spmd

    nc = bacc.Bacc("TRN2", target_bir_lowering=False, num_devices=1)
    arrays, args = {}, []
    for name in _INS:
        a = np.asarray(inputs[name])
        if name == "L0_ffn_expert_w":
            a = a.transpose(0, 2, 1)
        if name == "L0_ffn_gate_w":
            a = a.T
        if name in ("L0_attn_bq", "L0_attn_bk"):
            a = a.reshape(-1, P).T
        a = np.ascontiguousarray(a)
        arrays[f"in_{name}"] = a
        args.append(nc.dram_tensor(f"in_{name}", a.shape, mybir.dt.from_np(a.dtype), kind="ExternalInput").ap())
    out = nc.dram_tensor("out_y", arrays["in_L0_attn_x"].shape, F32, kind="ExternalOutput").ap()
    preln_attention_moe(nc, *args, out)
    r = run_bass_kernel_spmd(nc, [arrays], core_ids=[0])
    return r.results[0]["out_y"]
```

```python
from contextlib import ExitStack

import concourse.bass as bass
from concourse import mybir

ALU = mybir.AluOpType
ACT = mybir.ActivationFunctionType
AX = mybir.AxisListType
F32 = mybir.dt.float32
BF16 = mybir.dt.bfloat16
U32 = mybir.dt.uint32
F32R = mybir.dt.float32r

P = 128
EPS = 1e-5


def preln_attention_moe(nc, x, Wq, bq, Wk, bk, Wv, bv, Wo, bo, gate_w, expert_w, expert_b, out):
    _, T, D = x.shape
    E = gate_w.shape[1]
    KVD = Wk.shape[1]
    DK = 16
    G = KVD // DK
    REP = D // KVD
    KD = D // P
    CH = 512
    NC = T // CH
    TT = CH // P
    NKT = T // P
    NKC = T // CH
    N = G * NC
    SCALE = DK ** -0.5

    Q_PART = [0, 1, 2, 0, 1, 0]
    K_PART = [0, 0, 0, 1, 1, 2]
    NTERM = len(Q_PART)
    CROW = NTERM * DK
    SROW = CROW + 3

    SLOTS = 8
    LEAD = 2
    PRING = 16
    UNITS = NKT * REP
    SBANKS = [0, 1, 7]
    RING = [("score", u) for u in range(UNITS)]
    RING.insert(REP * 2 + 3, ("outputs", 0))
    RING.insert(REP * 5 + 4, ("maxima", 0))
    assert len(RING) % len(SBANKS) == 0
    MUNITS = REP * TT * NKC // 2

    q_parts = nc.dram_tensor("q_parts", [3, D, T], BF16).ap()
    k_parts = nc.dram_tensor("k_parts", [3, KVD, T], BF16).ap()
    heads_out = nc.dram_tensor("heads_out", [NC, P, TT, G + 1, REP * DK], F32).ap()

    x_t = x.rearrange("a (n p) d -> p (a n) d", p=P)
    out_t = out.rearrange("a (n p) d -> p (a n) d", p=P)

    with ExitStack() as ctx:
        def sb(name, shape, dt=F32):
            return ctx.enter_context(nc.sbuf_tensor(name, shape, dt))

        def sem(name):
            return ctx.enter_context(nc.semaphore(name))

        bank = ctx.enter_context(nc.psum_tensor("bank", [P, 8, CH], F32))

        v_cur = sb("v_cur", [P, NKT, 2 * DK])
        wo_hi = sb("wo_hi", [P, KD, D], F32R)
        wg_sb = sb("wg_sb", [P, KD, E])
        wg_hi = sb("wg_hi", [P, KD, E], F32R)
        wg_lo = sb("wg_lo", [P, KD, E], F32R)
        be_sb = sb("be_sb", [P, D])
        ident = sb("ident", [P, P])
        bq_sb = sb("bq_sb", [P, KD])
        bk_sb = sb("bk_sb", [P, 1])
        bo_sb = sb("bo_sb", [P, D])
        stats = sb("stats", [P, TT, 6])
        mv = sb("mv", [P, TT, 2])
        std = sb("std", [P, TT])
        rstd = sb("rstd", [P, TT])
        mv2 = sb("mv2", [P, NKT, 2])
        std2 = sb("std2", [P, NKT])
        rstd2 = sb("rstd2", [P, NKT])
        eps_sb = sb("eps_sb", [P, 1])
        exp_warm = sb("exp_warm", [P, 1])
        max_kc = sb("max_kc", [P, MUNITS])
        max_q = sb("max_q", [P, REP * TT])
        negmax = sb("negmax", [REP * TT, P])
        shift = sb("shift", [REP * TT, 3, P], BF16)
        o_acc = sb("o_acc", [P, CH])
        o_rec = sb("o_rec", [P, TT, REP, 1])
        o_norm = sb("o_norm", [P, TT, REP, DK])
        iota_f = sb("iota_f", [P, E])
        xn2 = sb("xn2", [P, 2, D])
        logits = sb("logits", [P, 2, E])
        top = sb("top", [P, 2, 8])
        top_i = sb("top_i", [P, 2, 8], U32)
        top_f = sb("top_f", [P, 2, 2])
        g_exp = sb("g_exp", [P, 2, 3])
        g_w = sb("g_w", [P, 2, 2])
        g_tmp = sb("g_tmp", [P, 2, E])
        g_pad = sb("g_pad", [P, 2, P])
        g_padT = sb("g_padT", [P, 2, P])

        def in_turn(*turns):
            made = []
            for turn in turns:
                with ExitStack() as stack:
                    made.append([stack.enter_context(nc.sbuf_tensor(name, shape, dt)) for name, shape, dt in turn])
            return made

        with nc.sbuf_tensor("we_raw", [P, E, KD, D], F32) as we_raw:
            pass
        we_lo = sb("we_lo", [P, E, KD, D], F32R)
        with nc.sbuf_tensor("wo_raw", [P, KD, D], F32) as wo_raw:
            pass
        wo_lo = sb("wo_lo", [P, KD, D], F32R)

        (arena_q, arena_k, arena_p, v_all), = in_turn(
            [("arena_q", [P, 8192], F32),
             ("arena_k", [P, 8192], F32),
             ("arena_p", [P, 8192], F32),
             ("v_all", [P, NKT, KVD], F32)])
        x2_all = sb("x2_all", [P, NKT, D])
        EA = 6
        we_hi_a = sb("we_hi_a", [P, EA, KD, D], F32R)
        (atT_hi, atT_lo, at), (we_hi_b, x2T_hi, x2T_lo) = in_turn(
            [("atT_hi", [P, 2, KD, P], F32R), ("atT_lo", [P, 2, KD, P], F32R),
             ("at", [P, 2, TT, D], F32)],
            [("we_hi_b", [P, E - EA, KD, D], F32R), ("x2T_hi", [P, 2, KD, P], F32R), ("x2T_lo", [P, 2, KD, P], F32R)])

        def we_hi(e):
            return we_hi_a[:, e, :, :] if e < EA else we_hi_b[:, e - EA, :, :]

        x_all = arena_q[:, 0:8192].rearrange("p (n d) -> p n d", d=D)
        qf = arena_k[:, 1792:4352].rearrange("p (u s) -> p u s", u=5)
        parts = arena_k[:, 4352:8192].bitcast(BF16).rearrange("p (u a s) -> p u a s", u=5, a=3)
        xn = arena_p[:, 0:2048].rearrange("p (n d) -> p n d", d=D)
        xT = arena_p[:, 2048:4096].rearrange("p (k s) -> p k s", k=KD)
        wq_sb = arena_p[:, 4096:6144].rearrange("p (k n) -> p k n", k=KD)
        wk_sb = arena_p[:, 6144:6656].rearrange("p (k n) -> p k n", k=KD)
        wv_sb = arena_p[:, 6656:7168].rearrange("p (k n) -> p k n", k=KD)
        bv_sb = arena_p[:, 7168:7680].rearrange("p (t n) -> p t n", t=TT)
        q_st = arena_q[:, :].bitcast(BF16).rearrange("p (c h s) -> p c h s", c=SLOTS, h=REP)
        q_flat = arena_q[:, :].bitcast(BF16)
        k_st = arena_k[:, :].bitcast(BF16).rearrange("p (g s) -> p g s", g=G)
        k_flat = arena_k[:, :].bitcast(BF16)
        probs = arena_p[:, :].rearrange("p (r s) -> p r s", r=PRING)
        x_dma = [sem(f"x_dma{c}") for c in range(NC)]
        x_ready = sem("x_ready")
        wa_dma = sem("wa_dma")
        wc_dma = sem("wc_dma")
        consts = sem("consts")
        ident_ready = sem("ident_ready")
        iota_ready = sem("iota_ready")
        pool_step = sem("pool_step")
        mv_ready = sem("mv_ready")
        std_ready = sem("std_ready")
        xn_ready = sem("xn_ready")
        t_full = sem("t_full")
        t_evac = sem("t_evac")
        proj_full = sem("proj_full")
        proj_evac = sem("proj_evac")
        v_full = sem("v_full")
        v_evac = sem("v_evac")
        hi_ready = sem("hi_ready")
        parts_ready = sem("parts_ready")
        parts_stored = sem("parts_stored")
        step_n = sem("step_n")
        step_s = sem("step_s")
        k0_dma = sem("k0_dma")
        kr_dma = sem("kr_dma")
        q_dma = sem("q_dma")
        s_full = sem("s_full")
        p_ready = sem("p_ready")
        pv_done = sem("pv_done")
        v_ready = sem("v_ready")
        m_full = sem("m_full")
        m_done = sem("m_done")
        maxq_ready = sem("maxq_ready")
        mT_full = sem("mT_full")
        neg_ready = sem("neg_ready")
        ones_ready = sem("ones_ready")
        step_m = sem("step_m")
        shift_ready = sem("shift_ready")
        shift_dma = sem("shift_dma")
        o_ready = sem("o_ready")
        oT_full = sem("oT_full")
        rec_ready = sem("rec_ready")
        onorm_ready = sem("onorm_ready")
        o_dma = sem("o_dma")
        at_dma = sem("at_dma")
        xr_dma = sem("xr_dma")
        xb_ready = sem("xb_ready")
        wo_split = sem("wo_split")
        we_split = sem("we_split")
        wlo_ready = sem("wlo_ready")
        elo_ready = sem("elo_ready")
        at_full = sem("at_full")
        at_hi = sem("at_hi")
        at_evac = sem("at_evac")
        wo_full = sem("wo_full")
        x2_ready = sem("x2_ready")
        step_c = sem("step_c")
        step_g = sem("step_g")
        mv2_ready = sem("mv2_ready")
        std2_ready = sem("std2_ready")
        xn2_ready = sem("xn2_ready")
        xt_full = sem("xt_full")
        xt_hi = sem("xt_hi")
        xt_evac = sem("xt_evac")
        gl_full = sem("gl_full")
        gl_evac = sem("gl_evac")
        gd_ready = sem("gd_ready")
        ge_ready = sem("ge_ready")
        gw_ready = sem("gw_ready")
        gT_full = sem("gT_full")
        gT_evac = sem("gT_evac")
        y_full = sem("y_full")
        y_done = sem("y_done")
        out_dma = sem("out_dma")

        sp_passed = sem("sp_passed")
        dve_passed = sem("dve_passed")

        YU = E + 1
        YR = 3

        def ring_bank(entry):
            return SBANKS[RING.index(entry) % len(SBANKS)]

        B_OUT, B_MAX = ring_bank(("outputs", 0)), ring_bank(("maxima", 0))

        block = ctx.enter_context(nc.Block())

        @block.gpsimd
        def _(pool):
            pool.memset(ident[:, :], 0.0).then_inc(pool_step, 1)
            pool.wait_ge(pool_step, 1)
            pool.affine_select(out=ident[:, :], in_=ident[:, :], compare_op=ALU.not_equal, fill=1.0,
                               base=0, pattern=[[-1, P]], channel_multiplier=1).then_inc(ident_ready, 1)
            pool.iota(iota_f[:, :], [[1, E]], base=0, channel_multiplier=0,
                      allow_small_or_imprecise_dtypes=True).then_inc(iota_ready, 1)
            pool.dma_start(wo_raw[:, :, :], Wo.rearrange("(k p) n -> p k n", p=P)).then_inc(wc_dma, 16)
            pool.dma_start(wg_sb[:, :, :], gate_w.rearrange("(k p) n -> p k n", p=P)).then_inc(wc_dma, 16)
            pool.wait_ge(consts, 4)
            pool.dma_start(be_sb[0:E, :], expert_b).then_inc(wc_dma, 16)
            pool.dma_start(bo_sb[:, :], bo.partition_broadcast(P)).then_inc(wc_dma, 16)
            for e in range(E):
                pool.dma_start(we_raw[:, e, :, :],
                               expert_w[e].rearrange("(k p) n -> p k n", p=P)).then_inc(wc_dma, 16)

            pool.wait_ge(ident_ready, 1)
            pool.wait_ge(iota_ready, 1)
            pool.memset(k_st[CROW:SROW, 0, :], 1.0).then_inc(ones_ready, 1)
            pool.wait_ge(parts_stored, 1 + 16 * 5 * NC)
            pool.wait_ge(ones_ready, 1)
            pool.memset(k_st[CROW:SROW, 1:G, :], 1.0).then_inc(ones_ready, 1)

            pool.wait_ge(ones_ready, 2)
            pool.wait_ge(v_evac, 1 + NC)
            with pool.Fori(0, G) as g:
                pool.wait_ge(pv_done, PRING // REP + NKT * NC * g)
                pool.tensor_copy(v_cur[:, :, 0:DK], v_all[:, :, bass.ds(g * DK, DK)]).then_inc(v_ready, 1)

            pool.wait_ge(wc_dma, 16 * (4 + E))
            pool.wait_ge(s_full, UNITS * N)
            for c in range(NC):
                pool.dma_start(x2_all[:, c * TT:(c + 1) * TT, :], x_t[:, c * TT:(c + 1) * TT, :]).then_inc(xr_dma, 16)
                pool.wait_ge(xr_dma, 16 * (c + 1))
                for t in range(TT):
                    tile = x2_all[:, c * TT + t, :]
                    pool.tensor_tensor(tile, tile, bo_sb[:, :], ALU.add).then_inc(xb_ready, 1)

        @block.sync
        def _(sp):
            for c in range(NC):
                if c == 1:
                    sp.wait_ge(x_dma[0], 16)
                    sp.sem_inc(x_ready, 1)
                sp.dma_start(x_all[:, c * TT:(c + 1) * TT, :], x_t[:, c * TT:(c + 1) * TT, :]).then_inc(x_dma[c], 16)
            for c in range(1, NC):
                sp.wait_ge(x_dma[c], 16)
                sp.sem_inc(x_ready, 1)

            def wait_first(s, value):
                sp.wait_ge(s, value)
                sp.sem_inc(sp_passed, 1)

            def store_parts(c, u):
                wait_first(parts_ready, 5 * c + u + 1)
                dst = k_parts if u == 0 else q_parts[:, (u - 1) * P:u * P, :]
                sp.dma_start(dst[:, :, bass.ds(c * CH, CH)].rearrange("a p s -> p a s"),
                             parts[:, u, :, :]).then_inc(parts_stored, 16)

            with sp.Fori(0, NC - 1) as c:
                for u in range(5):
                    store_parts(c, u)

            def load_keys(groups, done):
                for t in range(NTERM):
                    src = k_parts[K_PART[t]].rearrange("(g d) s -> d g s", d=DK)
                    sp.dma_start(k_st[t * DK:(t + 1) * DK, groups, :], src[:, groups, :]).then_inc(done, 16)

            def load_queries(j):
                g, qc, slot = j // NC, j % NC, j % SLOTS
                for t in range(NTERM):
                    src = q_parts[Q_PART[t]].rearrange("(f d) s -> d f s", d=DK)
                    sp.dma_start(q_st[t * DK:(t + 1) * DK, bass.ds(slot, 1), :, :].squeeze(1),
                                 src[:, bass.ds(g * REP, REP), bass.ds(qc * CH, CH)]).then_inc(q_dma, 16)
                wait_first(q_dma, 16 * NTERM * (j + 1))

            def place_shift(j):
                wait_first(shift_ready, j + 1)
                for a in range(3):
                    dst = q_st[CROW + a:CROW + a + 1, bass.ds(j % SLOTS, 1), :, :].squeeze(1)
                    sp.dma_start(dst.rearrange("o h (t q) -> o (h t) q", t=TT),
                                 shift[:, a, :]).then_inc(shift_dma, 16)
                wait_first(shift_dma, 1 + 48 * (j + 1))

            def store_heads(i):
                wait_first(onorm_ready, 1 + i + 1)
                slot = i + NC - 1
                dst = heads_out[bass.ds(slot % NC, 1)].squeeze(0)
                sp.dma_start(dst[:, :, bass.ds(slot // NC, 1), :].squeeze(2),
                             o_norm[:, :, :, :].rearrange("p t h d -> p t (h d)")).then_inc(o_dma, 16)

            store_parts(NC - 1, 0)
            sp.wait_ge(parts_stored, 1 + 16 * (5 * (NC - 1) + 1))
            load_keys(slice(0, 1), k0_dma)
            for j in range(LEAD):
                load_queries(j)
            for u in range(1, 5):
                store_parts(NC - 1, u)
            sp.wait_ge(parts_stored, 1 + 16 * 5 * NC)
            load_keys(slice(1, G), kr_dma)
            with sp.Fori(LEAD, SLOTS) as j:
                load_queries(j)
            place_shift(0)
            with sp.Fori(0, N - SLOTS) as i:
                store_heads(i)
                place_shift(i + 1)
                wait_first(s_full, UNITS * (i + 1))
                load_queries(i + SLOTS)
            with sp.Fori(N - SLOTS, N - 2) as i:
                store_heads(i)
                place_shift(i + 1)

            def load_heads(c):
                src = heads_out[bass.ds(c, 1)].squeeze(0)
                sp.dma_start(at[:, bass.ds((c + 1) % 2, 1), :, :].squeeze(1),
                             src[:, :, 1:G + 1, :].rearrange("p t g f -> p t (g f)")).then_inc(at_dma, 16)

            sp.wait_ge(o_dma, 1 + 16 * (N - 2))
            sp.wait_ge(v_ready, G)
            load_heads(0)
            store_heads(N - 2)
            place_shift(N - 1)
            for i in (N - 1, N):
                store_heads(i)

            sp.wait_ge(o_dma, 1 + 16 * (N + 1))
            sp.wait_ge(at_dma, 16)
            load_heads(1)
            with sp.Fori(2, NC) as c:
                wait_first(at_full, TT * (c - 1))
                wait_first(at_dma, 16 * c)
                load_heads(c)
            with sp.Fori(0, NKT) as n:
                wait_first(y_done, YR + YU * (n + 1))
                sp.dma_start(out_t[:, bass.ds(n, 1), :], x2_all[:, bass.ds(n, 1), :]).then_inc(out_dma, 16)
            sp.wait_ge(out_dma, 16 * NKT)

        @block.scalar
        def _(act):
            for s, n in ((t_evac, 2), (proj_evac, 5), (p_ready, 3)):
                act.sem_inc(s, n)
            act.dma_start(wk_sb[:, :, :], Wk.rearrange("(k p) n -> p k n", p=P)).then_inc(wa_dma, 16)
            act.dma_start(wq_sb[:, :, :], Wq.rearrange("(k p) n -> p k n", p=P)).then_inc(wa_dma, 16)
            act.dma_start(wv_sb[:, :, :], Wv.rearrange("(k p) n -> p k n", p=P)).then_inc(wa_dma, 16)
            act.dma_start(bq_sb[:, :], bq).then_inc(wa_dma, 16)
            act.dma_start(bk_sb[:, :], bk).then_inc(wa_dma, 16)
            for t in range(TT):
                act.dma_start(bv_sb[:, t, :], bv.partition_broadcast(P)).then_inc(wa_dma, 16)
            act.wait_ge(consts, 1)

            def evacuate_transposes(n, dst, t):
                act.wait_ge(t_full, n + 1)
                act.activation(dst[:, :, t * P:(t + 1) * P],
                               bank[:, 6 + t % 2, :].rearrange("p (k s) -> p k s", k=KD),
                               ACT.Copy).then_inc(t_evac, 1)

            def deviation(c):
                act.wait_ge(mv_ready, c + 1)
                act.activation(std[:, :], mv[:, :, 1], ACT.Sqrt, bias=eps_sb[:, 0:1]).then_inc(std_ready, 1)

            def project_chunk(c, last):
                for t in range(TT):
                    evacuate_transposes(c * TT + t, xT, t)
                act.wait_ge(wa_dma, 16 * 9)
                if not last:
                    deviation(c + 1)
                act.wait_ge(parts_stored, 1 + 16 * 5 * c)
                for u in range(5):
                    act.wait_ge(proj_full, 5 * c + u + 1)
                    bias = bk_sb[:, 0:1] if u == 0 else bq_sb[:, u - 1:u]
                    act.activation(qf[:, u, :], bank[:, u, :], ACT.Identity, bias=bias).then_inc(proj_evac, 1)
                    act.wait_ge(proj_evac, 5 + 5 * c + u + 1)
                    act.activation(parts[:, u, 0, :], qf[:, u, :], ACT.Copy).then_inc(hi_ready, 1)

            deviation(0)
            with act.Fori(0, NC - 1) as c:
                project_chunk(c, False)
            project_chunk(NC - 1, True)

            act.wait_ge(wc_dma, 16 * (4 + E))
            act.activation(wo_hi[:, :, :], wo_raw[:, :, :], ACT.Copy).then_inc(wo_split, 1)
            act.activation(wg_hi[:, :, :], wg_sb[:, :, :], ACT.Copy).then_inc(wo_split, 1)

            act.activation(exp_warm[:, :], eps_sb[:, :], ACT.Exp)
            def copy_outputs(i):
                act.wait_ge(pv_done, PRING // REP + NKT * i)
                act.activation(o_acc[:, :], bank[:, 6, :], ACT.Copy).then_inc(o_ready, 1)

            with act.Fori(0, N) as i:
                for u in range(UNITS):
                    if u == 3:
                        copy_outputs(i)
                    act.wait_ge(s_full, UNITS * i + u + 1)
                    if u % REP == 0:
                        act.wait_ge(pv_done, NKT * i + u // REP + 1)
                    act.activation(probs[:, u % PRING, :], bank[:, ring_bank(("score", u)), :],
                                   ACT.Exp, scale=SCALE).then_inc(p_ready, 1)

            copy_outputs(N)

            def hi(dst, src):
                return act.activation(dst, src, ACT.Copy)

            def expert_hi(e, dst):
                hi(dst, we_raw[:, bass.ds(e, 1), :, :].squeeze(1)).then_inc(we_split, 1)

            def attention_hi(c):
                for t in range(TT):
                    act.wait_ge(at_full, TT * c + t + 1)
                    hi(atT_hi[:, t % 2, :, :],
                       bank[:, 2 + t % 2, :].rearrange("p (k s) -> p k s", k=KD)).then_inc(at_hi, 1)

            act.wait_ge(pv_done, PRING // REP + NKT * N)
            with act.Fori(0, NC - 1) as c:
                attention_hi(c)
                for q in range(2):
                    expert_hi(2 * c + q, we_hi_a[:, bass.ds(2 * c + q, 1), :, :].squeeze(1))
            attention_hi(NC - 1)
            act.wait_ge(mv2_ready, NC)
            act.activation(std2[:, :], mv2[:, :, 1], ACT.Sqrt, bias=eps_sb[:, 0:1]).then_inc(std2_ready, 1)
            act.wait_ge(wo_full, NKT)
            for e in range(EA, E):
                hi(we_hi(e), we_raw[:, e, :, :]).then_inc(we_split, 1)

            def gate_tile(n, b):
                act.wait_ge(xt_full, n + 1)
                hi(x2T_hi[:, b, :, :], bank[:, 6, :].rearrange("p (k s) -> p k s", k=KD)).then_inc(xt_hi, 1)
                act.wait_ge(gd_ready, n + 1)
                act.activation(g_exp[:, b, 1:2], g_exp[:, b, 0:1], ACT.Exp).then_inc(ge_ready, 1)
                act.wait_ge(gT_full, n + 1)
                act.activation(g_padT[:, b, :], bank[:, 7, P:2 * P], ACT.Copy).then_inc(gT_evac, 1)

            with act.Fori(0, NKT // 2) as m:
                for b in range(2):
                    gate_tile(2 * m + b, b)

        @block.tensor
        def _(pe):
            pe.wait_ge(ident_ready, 1)
            pe.wait_ge(consts, 4)

            def transpose_tile(n, src, ready, t):
                pe.wait_ge(ready, n[0])
                pe.wait_ge(t_evac, n[1])
                for k in range(KD):
                    mm = pe.transpose(bank[:, 6 + t % 2, k * P:(k + 1) * P], src[:, t, k * P:(k + 1) * P], ident[:, :])
                mm.then_inc(t_full, 1)

            with pe.Fori(0, NC) as c:
                for t in range(TT):
                    transpose_tile((c * TT + t + 1, c * TT + t + 1), xn, xn_ready, t)
                pe.wait_ge(wa_dma, 16 * 9)
                pe.wait_ge(t_evac, 2 + TT * (c + 1))
                for u in range(5):
                    pe.wait_ge(proj_evac, 5 * c + u + 1)
                    for k in range(KD):
                        w = wk_sb[:, k, :] if u == 0 else wq_sb[:, k, (u - 1) * P:u * P]
                        mm = pe.matmul(bank[:, u, :], w, xT[:, k, :], start=(k == 0), stop=(k == KD - 1))
                    mm.then_inc(proj_full, 1)
                pe.wait_ge(v_evac, c + 1)
                for t in range(TT):
                    for k in range(KD):
                        mm = pe.matmul(bank[:, 5, t * KVD:(t + 1) * KVD], xT[:, k, t * P:(t + 1) * P],
                                       wv_sb[:, k, :], start=(k == 0), stop=(k == KD - 1))
                mm.then_inc(v_full, 1)

            def max_unit(j, m):
                h, qt, half = m // (2 * TT), m // 2 % TT, m % 2
                pe.wait_ge(m_done, MUNITS * j + m + 1)
                qo = (j % SLOTS) * (REP * CH) + h * CH + qt * P
                for q in range(2):
                    mm = pe.matmul(bank[:, 2 + 2 * (m % 2) + q, :], q_flat[0:CROW, bass.ds(qo, P)],
                                   k_flat[0:CROW, bass.ds((j // NC) * T + (2 * half + q) * CH, CH)],
                                   start=True, stop=True)
                mm.then_inc(m_full, 1)

            def max_transpose(j):
                pe.wait_ge(maxq_ready, j + 1)
                pe.transpose(bank[0:REP * TT, B_MAX, 0:P], max_q[:, :], ident[:, :]).then_inc(mT_full, 1)

            def ring_bank_free(i, entry):
                r = RING.index(entry) - len(SBANKS)
                kind, u = RING[r]
                if r < 0:
                    pe.wait_ge(p_ready, UNITS * i + u - UNITS + len(SBANKS) + 1)
                elif kind == "score":
                    pe.wait_ge(p_ready, len(SBANKS) + UNITS * i + u + 1)
                elif kind == "outputs":
                    pe.wait_ge(onorm_ready, 2 + i)
                else:
                    pe.wait_ge(neg_ready, min(i, N - 2) + 3 if isinstance(i, int) else i + 3)

            def score_unit(i, u):
                kt, h = u // REP, u % REP
                ring_bank_free(i, ("score", u))
                qo = (i % SLOTS) * (REP * CH) + h * CH
                pe.matmul(bank[:, ring_bank(("score", u)), :], k_flat[0:SROW, bass.ds((i // NC) * T + kt * P, P)],
                          q_flat[0:SROW, bass.ds(qo, CH)], start=True, stop=True).then_inc(s_full, 1)

            def value_product(i, kt):
                pe.wait_ge(p_ready, len(SBANKS) + UNITS * i + REP * (kt + 1))
                for h in range(REP):
                    mm = pe.matmul(bank[32 * h:32 * h + 32, 6, :], v_cur[:, kt, :],
                                   probs[:, (REP * kt + h) % PRING, :],
                                   start=(kt == 0), stop=(kt == NKT - 1))
                mm.then_inc(pv_done, 1)

            def output_transpose(i):
                pe.wait_ge(o_ready, i + 1)
                if isinstance(i, int) and i == N:
                    pe.wait_ge(p_ready, len(SBANKS) + UNITS * N)
                else:
                    ring_bank_free(i, ("outputs", 0))
                for t in range(TT):
                    mm = pe.transpose(bank[:, B_OUT, t * P:(t + 1) * P], o_acc[:, t * P:(t + 1) * P], ident[:, :])
                mm.then_inc(oT_full, 1)

            pe.wait_ge(proj_evac, 5 + 5 * NC)
            pe.wait_ge(v_evac, 1 + NC)
            pe.wait_ge(t_evac, 2 + NKT)
            pe.wait_ge(k0_dma, 16 * NTERM)
            for j in range(LEAD):
                pe.wait_ge(q_dma, 16 * NTERM * (j + 1))
                for m in range(MUNITS):
                    max_unit(j, m)
                if j < LEAD - 1:
                    max_transpose(j)
            pe.wait_ge(kr_dma, 16 * NTERM)
            pe.wait_ge(ones_ready, 2)

            def attention_step(i, kt, with_max, with_shift):
                score_unit(i, REP * kt)
                score_unit(i, REP * kt + 1)
                if with_max:
                    max_unit(i + LEAD, 2 * kt)
                score_unit(i, REP * kt + 2)
                if kt >= 1:
                    if kt == 1:
                        pe.wait_ge(v_ready, i // NC + 1)
                        pe.wait_ge(o_ready, i + 1)
                    value_product(i, kt - 1)
                elif not (isinstance(i, int) and i == 0):
                    value_product(i - 1, NKT - 1)
                if kt == 2:
                    output_transpose(i)
                if kt == 5 and with_shift:
                    ring_bank_free(i, ("maxima", 0))
                    max_transpose(i + 1)
                if with_max:
                    max_unit(i + LEAD, 2 * kt + 1)
                score_unit(i, REP * kt + 3)

            def first_step(i, with_max):
                pe.wait_ge(shift_dma, 1 + 48 * (i + 1))
                if with_max:
                    pe.wait_ge(q_dma, 16 * NTERM * (i + LEAD + 1))
                attention_step(i, 0, with_max, True)

            def other_steps(i, with_max, with_shift):
                for kt in range(1, NKT):
                    attention_step(i, kt, with_max, with_shift)

            first_step(0, True)
            with pe.Fori(0, N - LEAD - 1) as i:
                other_steps(i, True, True)
                first_step(i + 1, True)
            other_steps(N - LEAD - 1, True, True)
            for i in range(N - LEAD, N):
                first_step(i, False)
                other_steps(i, False, i < N - 1)
            value_product(N - 1, NKT - 1)
            output_transpose(N)

            def product(out_, lhs, rhs, first=True, last=True):
                terms = [(lhs[0], rhs[0]), (lhs[1], rhs[0]), (lhs[0], rhs[1])]
                for q, (a, w) in enumerate(terms):
                    for k in range(KD):
                        mm = pe.matmul(out_, a(k), w(k), start=(q == 0 and k == 0), stop=(q == 2 and k == KD - 1))
                return mm

            pe.wait_ge(m_done, 2 + MUNITS * N)
            pe.wait_ge(o_ready, N + 1)
            pe.wait_ge(p_ready, len(SBANKS) + UNITS * N)
            pe.wait_ge(wlo_ready, 2)
            def transpose_attention(n, t, half):
                pe.wait_ge(at_evac, n + 1)
                for k in range(KD):
                    mm = pe.transpose(bank[:, 2 + t % 2, k * P:(k + 1) * P], at[:, half, t, k * P:(k + 1) * P], ident[:, :])
                mm.then_inc(at_full, 1)

            def attention_chunk(c, half, last):
                for t in range(TT):
                    if t < TT - 1:
                        transpose_attention(c * TT + t + 1, t + 1, half)
                    elif not last:
                        pe.wait_ge(at_dma, 16 * (c + 2))
                        transpose_attention(c * TT + TT, 0, 1 - half)
                    pe.wait_ge(at_evac, 2 + TT * c + t + 1)
                    pe.wait_ge(x2_ready, TT * c + t + 1)
                    product(bank[:, 4 + t % 2, :],
                            [lambda k: atT_hi[:, t % 2, k, :], lambda k: atT_lo[:, t % 2, k, :]],
                            [lambda k: wo_hi[:, k, :], lambda k: wo_lo[:, k, :]]).then_inc(wo_full, 1)

            pe.wait_ge(at_dma, 16)
            transpose_attention(0, 0, 1)
            for c in range(NC):
                attention_chunk(c, (c + 1) % 2, c == NC - 1)

            def transpose_x(n, b):
                pe.wait_ge(xn2_ready, n + 1)
                for k in range(KD):
                    mm = pe.transpose(bank[:, 6, k * P:(k + 1) * P], xn2[:, b, k * P:(k + 1) * P], ident[:, :])
                mm.then_inc(xt_full, 1)

            def halves(b):
                return [lambda k: x2T_hi[:, b, k, :], lambda k: x2T_lo[:, b, k, :]]

            def gate_logits(n, b):
                pe.wait_ge(xt_evac, n + 1)
                product(bank[:, 7, 0:E], halves(b),
                        [lambda k: wg_hi[:, k, :], lambda k: wg_lo[:, k, :]]).then_inc(gl_full, 1)

            def transpose_gate(n, b):
                pe.wait_ge(gw_ready, n + 1)
                pe.transpose(bank[:, 7, P:2 * P], g_pad[:, b, :], ident[:, :]).then_inc(gT_full, 1)

            def expert(n, b, e):
                pe.wait_ge(y_done, YU * n + e + 1)
                product(bank[:, e % YR, :], halves(b),
                        [lambda k: we_hi(e)[:, k, :], lambda k: we_lo[:, e, k, :]]).then_inc(y_full, 1)

            def expert_tile(n, b, first, last):
                nb = 1 - b
                for e in range(E):
                    if e == 1 and first:
                        transpose_gate(0, 0)
                    if e == (2 if first else 0) and not last:
                        transpose_x(n + 1, nb)
                    if e == 4 and not last:
                        gate_logits(n + 1, nb)
                    if e == 6 and not last:
                        transpose_gate(n + 1, nb)
                    if first:
                        pe.wait_ge(elo_ready, e + 1)
                    expert(n, b, e)
                pe.wait_ge(gT_evac, n + 1)
                pe.wait_ge(y_done, YU * n + E + 1)
                pe.matmul(bank[:, E % YR, :], g_padT[:, b, :], be_sb[:, :], start=True, stop=True).then_inc(y_full, 1)

            pe.wait_ge(onorm_ready, N + 2)
            transpose_x(0, 0)
            gate_logits(0, 0)
            expert_tile(0, 0, True, False)
            expert_tile(1, 1, False, False)
            with pe.Fori(1, NKT // 2 - 1) as m:
                for b in range(2):
                    expert_tile(2 * m + b, b, False, False)
            expert_tile(NKT - 2, 0, False, False)
            expert_tile(NKT - 1, 1, False, True)

        @block.vector
        def _(dve):
            for s, n in ((v_evac, 1), (parts_stored, 1), (pv_done, PRING // REP), (m_done, 2), (neg_ready, 1),
                         (shift_dma, 1), (onorm_ready, 1), (o_dma, 1), (x2_ready, 2),
                         (at_evac, 2), (y_done, YR)):
                dve.sem_inc(s, n)
            dve.memset(eps_sb[:, :], EPS).then_inc(consts, 1)
            dve.memset(v_cur[:, :, DK:2 * DK], 1.0).then_inc(consts, 1)
            dve.memset(g_pad[:, :, :], 0.0).then_inc(consts, 1)
            dve.memset(be_sb[:, :], 0.0).then_inc(consts, 1)

            def chain(s, base):
                n = [0]

                def link(ins):
                    n[0] += 1
                    ins.then_inc(s, 1)
                    dve.wait_ge(s, base + n[0])
                    dve.sem_inc(dve_passed, 1)
                return link

            STEPS_N, STEPS_S = TT * 2 + 1, 5 * 2

            def normalise_chunk(c):
                link = chain(step_n, STEPS_N * c)
                dve.wait_ge(x_ready, c + 1)
                for t in range(TT):
                    link(dve.bn_stats(stats[:, t, :], x_all[:, bass.ds(c * TT + t, 1), :].squeeze(1)))
                for t in range(TT):
                    link(dve.bn_aggr(mv[:, t, :], stats[:, t, :]))
                dve.sem_inc(mv_ready, 1)
                dve.wait_ge(std_ready, c + 1)
                link(dve.reciprocal(rstd[:, :], std[:, :]))
                if not isinstance(c, int):
                    dve.wait_ge(t_full, TT * c)
                for t in range(TT):
                    dve.tensor_scalar(xn[:, t, :], x_all[:, bass.ds(c * TT + t, 1), :].squeeze(1), mv[:, t, 0:1],
                                      rstd[:, t:t + 1], ALU.subtract, ALU.mult).then_inc(xn_ready, 1)

            def split_chunk(c):
                link = chain(step_s, STEPS_S * c)
                for u in range(5):
                    dve.wait_ge(hi_ready, 5 * c + u + 1)
                    link(dve.tensor_tensor(qf[:, u, :], qf[:, u, :], parts[:, u, 0, :], ALU.subtract))
                    link(dve.tensor_copy(parts[:, u, 1, :], qf[:, u, :]))
                    dve.tensor_tensor(parts[:, u, 2, :], qf[:, u, :], parts[:, u, 1, :],
                                      ALU.subtract).then_inc(parts_ready, 1)
                dve.wait_ge(v_full, c + 1)
                dve.tensor_tensor(v_all[:, bass.ds(c * TT, TT), :], bank[:, 5, :].rearrange("p (t n) -> p t n", t=TT),
                                  bv_sb[:, :, :], ALU.add).then_inc(v_evac, 1)

            normalise_chunk(0)
            with dve.Fori(0, NC - 1) as c:
                normalise_chunk(c + 1)
                split_chunk(c)
            split_chunk(NC - 1)

            dve.wait_ge(wo_split, 2)
            dve.tensor_tensor(wo_lo[:, :, :], wo_raw[:, :, :], wo_hi[:, :, :], ALU.subtract).then_inc(wlo_ready, 1)
            dve.tensor_tensor(wg_lo[:, :, :], wg_sb[:, :, :], wg_hi[:, :, :], ALU.subtract).then_inc(wlo_ready, 1)
            dve.wait_ge(iota_ready, 1)

            def reduce_unit(j, m):
                dve.wait_ge(m_full, MUNITS * j + m + 1)
                dve.reduce_max(max_kc[:, m:m + 1], bank[:, 2 + 2 * (m % 2):4 + 2 * (m % 2), :].rearrange("p a s -> p (a s)"),
                               AX.X).then_inc(m_done, 1)

            def combine_max(j):
                dve.wait_ge(m_done, 2 + MUNITS * (j + 1))
                dve.reduce_max(max_q[:, :], max_kc[:, :].rearrange("p (r c) -> p r c", c=2),
                               AX.X).then_inc(maxq_ready, 1)

            def make_shift(j, part):
                base = 3 * j
                if part == 0:
                    dve.wait_ge(mT_full, j + 1)
                    dve.wait_ge(shift_dma, 1 + 48 * j)
                    dve.tensor_scalar(negmax[:, :], bank[0:REP * TT, B_MAX, 0:P], -1.0, None,
                                      ALU.mult).then_inc(neg_ready, 1)
                elif part == 1:
                    dve.wait_ge(neg_ready, 1 + j + 1)
                    dve.tensor_copy(shift[:, 0, :], negmax[:, :]).then_inc(step_m, 1)
                elif part == 2:
                    dve.wait_ge(step_m, base + 1)
                    dve.tensor_tensor(negmax[:, :], negmax[:, :], shift[:, 0, :], ALU.subtract).then_inc(step_m, 1)
                elif part == 3:
                    dve.wait_ge(step_m, base + 2)
                    dve.tensor_copy(shift[:, 1, :], negmax[:, :]).then_inc(step_m, 1)
                else:
                    dve.wait_ge(step_m, base + 3)
                    dve.tensor_tensor(shift[:, 2, :], negmax[:, :], shift[:, 1, :],
                                      ALU.subtract).then_inc(shift_ready, 1)

            def normalise(i):
                dve.wait_ge(oT_full, i + 1)
                dve.wait_ge(o_dma, 1 + 16 * i)
                o = bank[:, B_OUT, :].rearrange("p (t h f) -> p t h f", t=TT, h=REP)
                dve.reciprocal(o_rec[:, :, :, :], o[:, :, :, DK:DK + 1]).then_inc(rec_ready, 1)
                dve.wait_ge(rec_ready, i + 1)
                dve.tensor_tensor(o_norm[:, :, :, :], o[:, :, :, 0:DK], o_rec[:, :, :, :].to_broadcast([P, TT, REP, DK]),
                                  ALU.mult).then_inc(onorm_ready, 1)

            for j in range(LEAD):
                for m in range(MUNITS):
                    reduce_unit(j, m)
                combine_max(j)
                dve.wait_ge(maxq_ready, j + 1)
                if j < LEAD - 1:
                    for part in range(5):
                        make_shift(j, part)

            def round_(i, with_max, with_shift):
                for kt in range(NKT):
                    if with_max:
                        reduce_unit(i + LEAD, 2 * kt)
                    if kt == 2:
                        normalise(i)
                    if 5 <= kt < 10 and with_shift:
                        make_shift(i + 1, kt - 5)
                    if with_max:
                        reduce_unit(i + LEAD, 2 * kt + 1)
                if with_max:
                    combine_max(i + LEAD)
                    dve.wait_ge(maxq_ready, i + LEAD + 1)

            with dve.Fori(0, N - LEAD) as i:
                round_(i, True, True)
            round_(N - 2, False, True)
            round_(N - 1, False, False)
            normalise(N)

            def expert_lo(e, e_hi):
                dve.wait_ge(we_split, e + 1)
                dve.tensor_tensor(we_lo[:, bass.ds(e, 1), :, :].squeeze(1), we_raw[:, bass.ds(e, 1), :, :].squeeze(1), e_hi,
                                  ALU.subtract).then_inc(elo_ready, 1)

            def attention_lo(n, t):
                dve.wait_ge(at_hi, n + 1)
                dve.tensor_tensor(atT_lo[:, t % 2, :, :], bank[:, 2 + t % 2, :].rearrange("p (k s) -> p k s", k=KD),
                                  atT_hi[:, t % 2, :, :], ALU.subtract).then_inc(at_evac, 1)

            STEPS_C = TT * 2 + 1

            def attention_chunk(c, last):
                base = STEPS_C * c

                def passed(step):
                    dve.wait_ge(step_c, base + step)
                    dve.sem_inc(dve_passed, 1)

                for t in range(TT):
                    if not (last and t == TT - 1):
                        attention_lo(c * TT + t + 1, t + 1)
                    tile = x2_all[:, bass.ds(c * TT + t, 1), :].squeeze(1)
                    dve.wait_ge(wo_full, TT * c + t + 1)
                    dve.wait_ge(xb_ready, TT * c + t + 1)
                    dve.tensor_tensor(tile, bank[:, 4 + t % 2, :], tile, ALU.add).then_inc(x2_ready, 1)
                    if t == 0:
                        expert_lo(c, we_hi_a[:, bass.ds(c, 1), :, :].squeeze(1))
                    else:
                        passed(2 * t - 1)
                        dve.bn_aggr(mv[:, t - 1, :], stats[:, t - 1, :]).then_inc(step_c, 1)
                    dve.wait_ge(x2_ready, 2 + TT * c + t + 1)
                    dve.sem_inc(dve_passed, 1)
                    dve.bn_stats(stats[:, t, :], tile).then_inc(step_c, 1)
                passed(2 * TT - 1)
                dve.bn_aggr(mv[:, TT - 1, :], stats[:, TT - 1, :]).then_inc(step_c, 1)
                passed(2 * TT)
                dve.tensor_copy(mv2[:, bass.ds(c * TT, TT), :], mv[:, :, :]).then_inc(step_c, 1)
                passed(2 * TT + 1)
                dve.sem_inc(mv2_ready, 1)

            attention_lo(0, 0)
            with dve.Fori(0, NC - 1) as c:
                attention_chunk(c, False)
            attention_chunk(NC - 1, True)
            dve.wait_ge(std2_ready, 1)
            dve.reciprocal(rstd2[:, :], std2[:, :]).then_inc(step_c, 1)
            dve.wait_ge(step_c, STEPS_C * NC + 1)

            def normalise_tile(n, b):
                dve.tensor_scalar(xn2[:, b, :], x2_all[:, bass.ds(n, 1), :].squeeze(1),
                                  mv2[:, bass.ds(n, 1), 0], rstd2[:, bass.ds(n, 1)],
                                  ALU.subtract, ALU.mult).then_inc(xn2_ready, 1)
                dve.wait_ge(xt_hi, n + 1)
                dve.tensor_tensor(x2T_lo[:, b, :, :], bank[:, 6, :].rearrange("p (k s) -> p k s", k=KD),
                                  x2T_hi[:, b, :, :], ALU.subtract).then_inc(xt_evac, 1)

            STEPS_G = 8

            def gate_top2(n, b):
                link = chain(step_g, STEPS_G * n)
                dve.wait_ge(gl_full, n + 1)
                link(dve.tensor_copy(logits[:, b, :], bank[:, 7, 0:E]))
                link(dve.max(top[:, b, :], logits[:, b, :]))
                link(dve.max_index(top_i[:, b, :], top[:, b, :], logits[:, b, :]))
                dve.tensor_tensor(g_exp[:, b, 0:1], top[:, b, 1:2], top[:, b, 0:1], ALU.subtract).then_inc(gd_ready, 1)
                link(dve.tensor_copy(top_f[:, b, :], top_i[:, b, 0:2]))
                return link

            def gate_weights(n, b, link):
                dve.wait_ge(ge_ready, n + 1)
                link(dve.tensor_scalar(g_exp[:, b, 2:3], g_exp[:, b, 1:2], 1.0, None, ALU.add))
                link(dve.reciprocal(g_w[:, b, 0:1], g_exp[:, b, 2:3]))
                link(dve.tensor_tensor(g_w[:, b, 1:2], g_exp[:, b, 1:2], g_w[:, b, 0:1], ALU.mult))
                dve.tensor_scalar(g_tmp[:, b, :], iota_f[:, :], top_f[:, b, 1:2], g_w[:, b, 1:2],
                                  ALU.is_equal, ALU.mult)
                link(dve.tensor_scalar(g_pad[:, b, 0:E], iota_f[:, :], top_f[:, b, 0:1], g_w[:, b, 0:1],
                                       ALU.is_equal, ALU.mult))
                dve.tensor_tensor(g_pad[:, b, 0:E], g_pad[:, b, 0:E], g_tmp[:, b, :], ALU.add).then_inc(gw_ready, 1)

            def add_expert(n, b, e):
                tile = x2_all[:, bass.ds(n, 1), :].squeeze(1)
                dve.wait_ge(y_full, YU * n + e + 1)
                dve.wait_ge(y_done, YR + YU * n + e)
                dve.scalar_tensor_tensor(tile, bank[:, e % YR, :], g_pad[:, b, e:e + 1], tile,
                                         ALU.mult, ALU.add).then_inc(y_done, 1)

            def expert_tile(n, b, first, last):
                nb = 1 - b
                dve.wait_ge(gw_ready, n + 1)
                if not last:
                    normalise_tile(n + 1, nb)
                for e in range(E):
                    if first and e < E - 4:
                        expert_lo(e + 4, we_hi(e + 4))
                    add_expert(n, b, e)
                    if e == 3 and not last:
                        link = gate_top2(n + 1, nb)
                    if e == 4 and not last:
                        gate_weights(n + 1, nb, link)
                tile = x2_all[:, bass.ds(n, 1), :].squeeze(1)
                dve.wait_ge(y_full, YU * n + E + 1)
                dve.wait_ge(y_done, YR + YU * n + E)
                dve.tensor_tensor(tile, bank[:, E % YR, :], tile, ALU.add).then_inc(y_done, 1)

            normalise_tile(0, 0)
            gate_weights(0, 0, gate_top2(0, 0))
            expert_tile(0, 0, True, False)
            expert_tile(1, 1, False, False)
            with dve.Fori(1, NKT // 2 - 1) as m:
                for b in range(2):
                    expert_tile(2 * m + b, b, False, False)
            expert_tile(NKT - 2, 0, False, False)
            expert_tile(NKT - 1, 1, False, True)


_INS = ["L0_attn_x", "L0_attn_Wq", "L0_attn_bq", "L0_attn_Wk", "L0_attn_bk", "L0_attn_Wv", "L0_attn_bv",
        "L0_attn_Wo", "L0_attn_bo", "L0_ffn_gate_w", "L0_ffn_expert_w", "L0_ffn_expert_b"]


def kernel(**inputs):
    import numpy as np
    import concourse.bacc as bacc
    from concourse.bass_utils import run_bass_kernel_spmd

    nc = bacc.Bacc("TRN2", target_bir_lowering=False, num_devices=1)
    arrays, args = {}, []
    for name in _INS:
        a = np.asarray(inputs[name])
        if name == "L0_ffn_expert_w":
            a = a.transpose(0, 2, 1)
        if name == "L0_ffn_gate_w":
            a = a.T
        if name in ("L0_attn_bq", "L0_attn_bk"):
            a = a.reshape(-1, P).T
        a = np.ascontiguousarray(a)
        arrays[f"in_{name}"] = a
        args.append(nc.dram_tensor(f"in_{name}", a.shape, mybir.dt.from_np(a.dtype), kind="ExternalInput").ap())
    out = nc.dram_tensor("out_y", arrays["in_L0_attn_x"].shape, F32, kind="ExternalOutput").ap()
    preln_attention_moe(nc, *args, out)
    r = run_bass_kernel_spmd(nc, [arrays], core_ids=[0])
    return r.results[0]["out_y"]
```

```python
from contextlib import ExitStack

import concourse.bass as bass
from concourse import mybir

ALU = mybir.AluOpType
ACT = mybir.ActivationFunctionType
AX = mybir.AxisListType
F32 = mybir.dt.float32
BF16 = mybir.dt.bfloat16
U32 = mybir.dt.uint32
F32R = mybir.dt.float32r

P = 128
EPS = 1e-5


def preln_attention_moe(nc, x, Wq, bq, Wk, bk, Wv, bv, Wo, bo, gate_w, expert_w, expert_b, out):
    _, T, D = x.shape
    E = gate_w.shape[1]
    KVD = Wk.shape[1]
    DK = 16
    G = KVD // DK
    REP = D // KVD
    KD = D // P
    CH = 512
    NC = T // CH
    TT = CH // P
    NKT = T // P
    NKC = T // CH
    N = G * NC
    SCALE = DK ** -0.5

    Q_PART = [0, 1, 2, 0, 1, 0]
    K_PART = [0, 0, 0, 1, 1, 2]
    NTERM = len(Q_PART)
    CROW = NTERM * DK
    SROW = CROW + 3

    PROJ = [(0, 0)] + [(0, u) for u in range(1, 5)] + [(c, 0) for c in range(1, NC)]
    EARLY = len(PROJ)
    PROJ += [(c, u) for c in range(1, NC) for u in range(1, 5)]
    PROJ_BANK = [u if p < EARLY else [0, 1, 6, 7][u - 1] for p, (c, u) in enumerate(PROJ)]

    SLOTS = 8
    SPLIT, MAX_T = 9, 10
    PRING = 16
    UNITS = NKT * REP
    SBANKS = [0, 1, 7]
    RING = [("score", u) for u in range(UNITS)]
    RING.insert(REP * 2 + 3, ("outputs", 0))
    RING.insert(REP * MAX_T + 4, ("maxima", 0))
    assert len(RING) % len(SBANKS) == 0
    MUNITS = REP * TT * NKC // 2
    AHEAD = MUNITS - 2 * SPLIT

    def maximum_of(i, kt):
        return (i + 1, AHEAD + 2 * kt) if kt < SPLIT else (i + 2, 2 * (kt - SPLIT))

    NS = 2 * T // P + E - 1
    SR = 4

    slots_x = nc.dram_tensor("slots_x", [NS * P, D], F32).ap()
    slots_y = nc.dram_tensor("slots_y", [NS * P, D], F32).ap()
    q_parts = nc.dram_tensor("q_parts", [3, D, T], BF16).ap()
    k_parts = nc.dram_tensor("k_parts", [3, KVD, T], BF16).ap()
    heads_out = nc.dram_tensor("heads_out", [NC, P, TT, G + 1, REP * DK], F32).ap()

    x_t = x.rearrange("a (n p) d -> p (a n) d", p=P)
    out_t = out.rearrange("a (n p) d -> p (a n) d", p=P)

    with ExitStack() as ctx:
        def sb(name, shape, dt=F32):
            return ctx.enter_context(nc.sbuf_tensor(name, shape, dt))

        def sem(name):
            return ctx.enter_context(nc.semaphore(name))

        bank = ctx.enter_context(nc.psum_tensor("bank", [P, 8, CH], F32))

        v_cur = sb("v_cur", [P, NKT, 2 * DK])
        wg_sb = sb("wg_sb", [P, KD, E])
        be_sb = sb("be_sb", [P, D])
        ident = sb("ident", [P, P])
        bq_sb = sb("bq_sb", [P, KD])
        bk_sb = sb("bk_sb", [P, 1])
        bo_sb = sb("bo_sb", [P, D])
        ones = sb("ones", [P, P])
        before = sb("before", [P, P])
        before_tile = sb("before_tile", [P, NKT + 1, E])
        upto = sb("upto", [P, E, E])
        rev = sb("rev", [P, NKT, E])
        steps128 = sb("steps128", [P, E, NKT])
        slot_no = sb("slot_no", [1, NS, E])
        stats = sb("stats", [P, TT, 6])
        mv = sb("mv", [P, TT, 2])
        std = sb("std", [P, TT])
        rstd = sb("rstd", [P, TT])
        mv2 = sb("mv2", [P, NKT, 2])
        std2 = sb("std2", [P, NKT])
        rstd2 = sb("rstd2", [P, NKT])
        eps_sb = sb("eps_sb", [P, 1])
        table_warm = sb("table_warm", [P, 2])
        max_kc = sb("max_kc", [P, MUNITS])
        max_q = sb("max_q", [P, REP * TT])
        negmax = sb("negmax", [REP * TT, P])
        shift = sb("shift", [REP * TT, 3, P], BF16)
        o_acc = sb("o_acc", [P, CH])
        o_rec = sb("o_rec", [P, TT, REP, 1])
        o_norm = sb("o_norm", [P, TT, REP, DK])
        gates = sb("gates", [P, NKT, E])
        g_w = sb("g_w", [P, 2, NKT, 1])
        slot_i = sb("slot_i", [P, 2, NKT], U32)
        expert_i = sb("expert_i", [1, NS], U32)
        g_pad = sb("g_pad", [P, 2, P])
        g_padT = sb("g_padT", [P, 2, P])

        def in_turn(*turns):
            made = []
            for turn in turns:
                with ExitStack() as stack:
                    made.append([stack.enter_context(nc.sbuf_tensor(name, shape, dt)) for name, shape, dt in turn])
            return made

        with nc.sbuf_tensor("xT", [P, NC, KD, CH], F32) as xT:
            pass
        with nc.sbuf_tensor("we_raw", [P, E, KD, D], F32) as we_raw:
            pass
        we_lo = sb("we_lo", [P, E, KD, D], F32R)
        ((wo_raw, wo_hi), (wo_lo,), (xn2, logits, logits2, pick, first, second, chosen, top, g_exp, totals, counts,
                                     tiles_of, grid, grid8, slot_f, expert_cmp, expert_f)) = in_turn(
            [("wo_raw", [P, KD, D], F32), ("wo_hi", [P, KD, D], F32R)],
            [("wo_lo", [P, KD, D], F32R)],
            [("xn2", [P, SR, D], F32),
             ("logits", [P, NKT, E], F32),
             ("logits2", [P, NKT, E], F32),
             ("pick", [P, NKT, E], F32),
             ("first", [P, NKT, E], F32),
             ("second", [P, NKT, E], F32),
             ("chosen", [P, NKT + 1, E], F32),
             ("top", [P, 4, NKT, 1], F32),
             ("g_exp", [P, 3, NKT, 1], F32),
             ("totals", [P, P], F32),
             ("counts", [P, E], F32),
             ("tiles_of", [P, 3, E], F32),
             ("grid", [P, E, NKT], F32),
             ("grid8", [P, E, E], F32),
             ("slot_f", [P, 2, NKT], F32),
             ("expert_cmp", [1, NS, E], F32),
             ("expert_f", [1, NS], F32)])
        xs = sb("xs", [P, SR, D])
        ys = sb("ys", [P, SR, D])

        (arena_q, arena_k, arena_p, v_all), = in_turn(
            [("arena_q", [P, 8192], F32),
             ("arena_k", [P, 8192], F32),
             ("arena_p", [P, 8192], F32),
             ("v_all", [P, NKT, KVD], F32)])
        x2_all = sb("x2_all", [P, NKT, D])
        EA = 4
        (_, xg, xgT, lgT, _, atT_hi, atT_lo, at), (we_hi, x2T_hi, x2T_lo) = in_turn(
            [("we_hi_early", [P, EA, KD, D], F32R),
             ("xg", [P, 2, D], F32), ("xgT", [P, 2, KD, P], F32),
             ("lgT", [E, CH], F32),
             ("spare", [P, 3 * D], F32),
             ("atT_hi", [P, 2, KD, P], F32R), ("atT_lo", [P, 2, KD, P], F32R),
             ("at", [P, 2, TT, D], F32)],
            [("we_hi", [P, E, KD, D], F32R), ("x2T_hi", [P, 2, KD, P], F32R), ("x2T_lo", [P, 2, KD, P], F32R)])

        x_all = arena_q[:, 0:8192].rearrange("p (n d) -> p n d", d=D)
        qf = arena_k[:, 1792:4352].rearrange("p (u s) -> p u s", u=5)
        parts = arena_k[:, 4352:8192].bitcast(BF16).rearrange("p (u a s) -> p u a s", u=5, a=3)
        xn = arena_p[:, 0:2048].rearrange("p (n d) -> p n d", d=D)
        wq_sb = arena_p[:, 4096:6144].rearrange("p (k n) -> p k n", k=KD)
        wk_sb = arena_p[:, 6144:6656].rearrange("p (k n) -> p k n", k=KD)
        wv_sb = arena_p[:, 6656:7168].rearrange("p (k n) -> p k n", k=KD)
        bv_sb = arena_p[:, 7168:7680].rearrange("p (t n) -> p t n", t=TT)
        q_st = arena_q[:, :].bitcast(BF16).rearrange("p (c h s) -> p c h s", c=SLOTS, h=REP)
        q_flat = arena_q[:, :].bitcast(BF16)
        k_st = arena_k[:, :].bitcast(BF16).rearrange("p (g s) -> p g s", g=G)
        k_flat = arena_k[:, :].bitcast(BF16)
        probs = arena_p[:, :].rearrange("p (r s) -> p r s", r=PRING)
        x0_dma = [sem(f"x0_dma{t}") for t in range(TT)]
        x_dma = [sem(f"x_dma{c}") for c in range(NC)]
        x_ready = sem("x_ready")
        wa_dma = sem("wa_dma")
        wo_dma = sem("wo_dma")
        wc_dma = sem("wc_dma")
        consts = sem("consts")
        ident_ready = sem("ident_ready")
        eye_ready = sem("eye_ready")
        pool_step = sem("pool_step")
        mv_ready = sem("mv_ready")
        std_ready = sem("std_ready")
        xn_ready = sem("xn_ready")
        t_full = sem("t_full")
        t_evac = sem("t_evac")
        proj_full = sem("proj_full")
        proj_evac = sem("proj_evac")
        v_full = sem("v_full")
        v_evac = sem("v_evac")
        hi_ready = sem("hi_ready")
        split_step = sem("split_step")
        parts_ready = sem("parts_ready")
        parts_stored = sem("parts_stored")
        step_n = sem("step_n")
        k0_dma = sem("k0_dma")
        kr_dma = sem("kr_dma")
        q_dma = sem("q_dma")
        s_full = sem("s_full")
        p_ready = sem("p_ready")
        pv_done = sem("pv_done")
        v_ready = sem("v_ready")
        m_full = sem("m_full")
        m_done = sem("m_done")
        maxq_ready = sem("maxq_ready")
        mT_full = sem("mT_full")
        neg_ready = sem("neg_ready")
        ones_ready = sem("ones_ready")
        step_m = sem("step_m")
        shift_ready = sem("shift_ready")
        shift_dma = sem("shift_dma")
        o_ready = sem("o_ready")
        oT_full = sem("oT_full")
        rec_ready = sem("rec_ready")
        onorm_ready = sem("onorm_ready")
        o_dma = sem("o_dma")
        at_dma = sem("at_dma")
        xr_dma = sem("xr_dma")
        xb_ready = sem("xb_ready")
        wo_split = sem("wo_split")
        we_split = sem("we_split")
        wlo_ready = sem("wlo_ready")
        elo_ready = sem("elo_ready")
        at_full = sem("at_full")
        at_hi = sem("at_hi")
        at_evac = sem("at_evac")
        wo_full = sem("wo_full")
        x2_ready = sem("x2_ready")
        step_c = sem("step_c")
        mv2_ready = sem("mv2_ready")
        std2_ready = sem("std2_ready")
        xg_ready = sem("xg_ready")
        gt_full = sem("gt_full")
        gt_evac = sem("gt_evac")
        lg_full = sem("lg_full")
        lgT_ready = sem("lgT_ready")
        xn2_ready = sem("xn2_ready")
        xt_full = sem("xt_full")
        xt_hi = sem("xt_hi")
        xt_evac = sem("xt_evac")
        gl_full = sem("gl_full")
        step_g = sem("step_g")
        gd_ready = sem("gd_ready")
        ge_ready = sem("ge_ready")
        chosen_ready = sem("chosen_ready")
        tot_full = sem("tot_full")
        tot_ready = sem("tot_ready")
        rank_full = sem("rank_full")
        slots_ready = sem("slots_ready")
        expert_ready = sem("expert_ready")
        zero_dma = sem("zero_dma")
        sc_dma = [sem(f"sc_dma{b}") for b in range(SR)]
        gw_ready = sem("gw_ready")
        gT_full = sem("gT_full")
        gT_evac = sem("gT_evac")
        bias_full = sem("bias_full")
        bias_done = sem("bias_done")
        xs_dma = [sem(f"xs_dma{b}") for b in range(SR)]
        y_full = sem("y_full")
        y_evac = sem("y_evac")
        ys_dma = [sem(f"ys_dma{b}") for b in range(SR)]
        yt_dma = [sem(f"yt_dma{b}") for b in range(SR)]
        sum1 = sem("sum1")
        sum2 = sem("sum2")
        out_dma = sem("out_dma")

        sp_passed = sem("sp_passed")
        dve_passed = sem("dve_passed")

        def ring_bank(entry):
            return SBANKS[RING.index(entry) % len(SBANKS)]

        B_OUT, B_MAX = ring_bank(("outputs", 0)), ring_bank(("maxima", 0))

        block = ctx.enter_context(nc.Block())

        @block.gpsimd
        def _(pool):
            pool.memset(ident[:, :], 0.0).then_inc(pool_step, 1)
            pool.wait_ge(pool_step, 1)
            pool.affine_select(out=ident[:, :], in_=ident[:, :], compare_op=ALU.not_equal, fill=1.0,
                               base=0, pattern=[[-1, P]], channel_multiplier=1).then_inc(ident_ready, 1)
            pool.memset(ones[:, :], 1.0).then_inc(pool_step, 1)
            pool.memset(before[:, :], 1.0).then_inc(pool_step, 1)
            pool.memset(upto[:, :, :], 1.0).then_inc(pool_step, 1)
            pool.wait_ge(pool_step, 4)
            pool.affine_select(out=before[:, :], in_=before[:, :], compare_op=ALU.is_gt, fill=0.0,
                               base=0, pattern=[[1, P]], channel_multiplier=-1).then_inc(pool_step, 1)
            pool.affine_select(out=upto[:, :, :], in_=upto[:, :, :], compare_op=ALU.is_ge, fill=0.0,
                               base=0, pattern=[[1, E], [-1, E]], channel_multiplier=0).then_inc(pool_step, 1)
            pool.iota(rev[:, :, :], [[0, NKT], [-1, E]], base=E, channel_multiplier=0,
                      allow_small_or_imprecise_dtypes=True).then_inc(pool_step, 1)
            pool.iota(steps128[:, :, :], [[0, E], [P, NKT]], base=0, channel_multiplier=0,
                      allow_small_or_imprecise_dtypes=True).then_inc(pool_step, 1)
            pool.iota(slot_no[:, :, :], [[1, NS], [0, E]], base=0, channel_multiplier=0,
                      allow_small_or_imprecise_dtypes=True).then_inc(pool_step, 1)
            pool.wait_ge(eye_ready, 1)
            pool.affine_select(out=before_tile[:, :, :], in_=before_tile[:, :, :], compare_op=ALU.is_gt, fill=0.0,
                               base=0, pattern=[[E, NKT + 1], [0, E]], channel_multiplier=-1).then_inc(pool_step, 1)
            pool.dma_start(wo_raw[:, :, :], Wo.rearrange("(k p) n -> p k n", p=P)).then_inc(wo_dma, 16)
            pool.wait_ge(pool_step, 10)
            pool.wait_ge(ident_ready, 1)
            pool.memset(k_st[CROW:SROW, 0, :], 1.0).then_inc(ones_ready, 1)
            pool.wait_ge(ones_ready, 1)

            def place_values(g):
                pool.tensor_copy(v_cur[:, :, 0:DK], v_all[:, :, bass.ds(g * DK, DK)]).then_inc(v_ready, 1)

            for p, (c, u) in enumerate(PROJ):
                if p == EARLY + 4:
                    pool.wait_ge(parts_ready, p)
                    pool.wait_ge(v_evac, NC)
                    place_values(0)
                    pool.wait_ge(v_ready, 1)
                pool.wait_ge(hi_ready, p + 1)
                pool.tensor_tensor(qf[:, u, :], qf[:, u, :], parts[:, u, 0, :], ALU.subtract).then_inc(split_step, 1)
                pool.wait_ge(split_step, 2 * p + 1)
                pool.tensor_copy(parts[:, u, 1, :], qf[:, u, :]).then_inc(split_step, 1)
                pool.wait_ge(split_step, 2 * p + 2)
                pool.tensor_tensor(parts[:, u, 2, :], qf[:, u, :], parts[:, u, 1, :], ALU.subtract).then_inc(parts_ready, 1)

            pool.wait_ge(parts_stored, 16 * len(PROJ))
            pool.memset(k_st[CROW:SROW, 1:G, :], 1.0).then_inc(ones_ready, 1)

            pool.wait_ge(consts, 4)
            for z in range(NS):
                pool.dma_start(slots_x[z * P:(z + 1) * P, :], be_sb[:, :]).then_inc(zero_dma, 16)
                pool.wait_ge(zero_dma, 16 * (z + 1))
            pool.dma_start(be_sb[0:E, :], expert_b).then_inc(wc_dma, 16)
            pool.dma_start(bo_sb[:, :], bo.partition_broadcast(P)).then_inc(wc_dma, 16)
            pool.dma_start(wg_sb[:, :, :], gate_w.rearrange("(k p) n -> p k n", p=P)).then_inc(wc_dma, 16)
            pool.wait_ge(proj_full, len(PROJ))

            def load_expert(e):
                pool.dma_start(we_raw[:, bass.ds(e, 1), :, :].squeeze(1),
                               expert_w[bass.ds(e, 1)].squeeze(0).rearrange("(k p) n -> p k n", p=P)).then_inc(wc_dma, 16)

            load_expert(0)
            pool.wait_ge(ones_ready, 2)
            assert E == G
            with pool.Fori(1, G) as g:
                pool.wait_ge(pv_done, PRING // REP + NKT * NC * g)
                place_values(g)
                load_expert(g)

            pool.wait_ge(wc_dma, 16 * (3 + E))
            pool.wait_ge(s_full, UNITS * N)
            for c in range(NC):
                pool.dma_start(x2_all[:, c * TT:(c + 1) * TT, :], x_t[:, c * TT:(c + 1) * TT, :]).then_inc(xr_dma, 16)
                pool.wait_ge(xr_dma, 16 * (c + 1))
                for t in range(TT):
                    tile = x2_all[:, c * TT + t, :]
                    pool.tensor_tensor(tile, tile, bo_sb[:, :], ALU.add).then_inc(xb_ready, 1)

            pool.wait_ge(slots_ready, 1)
            for n in range(NKT):
                pool.wait_ge(xn2_ready, n + 1)
                for a in range(2):
                    pool.indirect_dma_start(slots_x, bass.IndirectOffsetOnAxis(ap=slot_i[:, a, n:n + 1], axis=0),
                                            xn2[:, n % SR, :], None).then_inc(sc_dma[n % SR], 16)
            for b in range(SR):
                pool.wait_ge(ys_dma[b], 16 * (len(range(b, NS, SR)) + 1))
            pool.wait_ge(xt_evac, 2 + NS)
            for n in range(NKT):
                pool.wait_ge(sum2, n + 1)
                for a, buf in enumerate((xs, ys)):
                    pool.indirect_dma_start(buf[:, n % SR, :], None, slots_y,
                                            bass.IndirectOffsetOnAxis(ap=slot_i[:, a, n:n + 1],
                                                                      axis=0)).then_inc(yt_dma[n % SR], 16)

        @block.sync
        def _(sp):
            for t in range(TT):
                sp.dma_start(x_all[:, t, :], x_t[:, t, :]).then_inc(x0_dma[t], 16)
            for t in range(TT):
                sp.wait_ge(x0_dma[t], 16)
                sp.sem_inc(x_ready, 1)
            sp.wait_ge(wa_dma, 16 * 9)
            for c in range(1, NC):
                sp.dma_start(x_all[:, c * TT:(c + 1) * TT, :], x_t[:, c * TT:(c + 1) * TT, :]).then_inc(x_dma[c], 16)
            for c in range(1, NC):
                sp.wait_ge(x_dma[c], 16)
                sp.sem_inc(x_ready, 1)

            def wait_first(s, value):
                sp.wait_ge(s, value)
                sp.sem_inc(sp_passed, 1)

            def store_parts(p):
                c, u = PROJ[p]
                sp.wait_ge(parts_ready, p + 1)
                dst = k_parts if u == 0 else q_parts[:, (u - 1) * P:u * P, :]
                sp.dma_start(dst[:, :, c * CH:(c + 1) * CH].rearrange("a p s -> p a s"),
                             parts[:, u, :, :]).then_inc(parts_stored, 16)

            def load_keys(groups, done):
                for t in range(NTERM):
                    src = k_parts[K_PART[t]].rearrange("(g d) s -> d g s", d=DK)
                    sp.dma_start(k_st[t * DK:(t + 1) * DK, groups, :], src[:, groups, :]).then_inc(done, 16)

            def load_queries(j):
                g, qc, slot = j // NC, j % NC, j % SLOTS
                for t in range(NTERM):
                    src = q_parts[Q_PART[t]].rearrange("(f d) s -> d f s", d=DK)
                    sp.dma_start(q_st[t * DK:(t + 1) * DK, bass.ds(slot, 1), :, :].squeeze(1),
                                 src[:, bass.ds(g * REP, REP), bass.ds(qc * CH, CH)]).then_inc(q_dma, 16)
                wait_first(q_dma, 16 * NTERM * (j + 1))

            def place_shift(j):
                wait_first(shift_ready, j + 1)
                for a in range(3):
                    dst = q_st[CROW + a:CROW + a + 1, bass.ds(j % SLOTS, 1), :, :].squeeze(1)
                    sp.dma_start(dst.rearrange("o h (t q) -> o (h t) q", t=TT),
                                 shift[:, a, :]).then_inc(shift_dma, 16)
                wait_first(shift_dma, 1 + 48 * (j + 1))

            def store_heads(i):
                wait_first(onorm_ready, 1 + i + 1)
                slot = i + NC - 1
                dst = heads_out[bass.ds(slot % NC, 1)].squeeze(0)
                sp.dma_start(dst[:, :, bass.ds(slot // NC, 1), :].squeeze(2),
                             o_norm[:, :, :, :].rearrange("p t h d -> p t (h d)")).then_inc(o_dma, 16)

            for p in range(EARLY):
                store_parts(p)
            sp.wait_ge(parts_stored, 16 * EARLY)
            load_keys(slice(0, 1), k0_dma)
            load_queries(0)
            for c in range(1, NC):
                for p in range(EARLY + 4 * (c - 1), EARLY + 4 * c):
                    store_parts(p)
                if c == NC - 2:
                    place_shift(0)
                sp.wait_ge(parts_stored, 16 * (EARLY + 4 * c))
                load_queries(c)
            load_keys(slice(1, G), kr_dma)
            load_queries(NC)
            store_heads(0)
            place_shift(1)
            with sp.Fori(NC + 1, SLOTS) as j:
                load_queries(j)
            wait_first(s_full, UNITS)
            load_queries(SLOTS)
            with sp.Fori(1, N - SLOTS) as i:
                store_heads(i)
                place_shift(i + 1)
                wait_first(s_full, UNITS * (i + 1))
                load_queries(i + SLOTS)
            with sp.Fori(N - SLOTS, N - 2) as i:
                store_heads(i)
                place_shift(i + 1)

            def load_heads(c):
                src = heads_out[bass.ds(c, 1)].squeeze(0)
                sp.dma_start(at[:, bass.ds((c + 1) % 2, 1), :, :].squeeze(1),
                             src[:, :, 1:G + 1, :].rearrange("p t g f -> p t (g f)")).then_inc(at_dma, 16)

            sp.wait_ge(o_dma, 1 + 16 * (N - 2))
            sp.wait_ge(v_ready, G)
            load_heads(0)
            store_heads(N - 2)
            place_shift(N - 1)
            store_heads(N - 1)
            sp.wait_ge(o_dma, 1 + 16 * N)
            sp.wait_ge(at_dma, 16)
            sp.wait_ge(pv_done, PRING // REP + NKT * N)
            load_heads(1)
            store_heads(N)

            sp.wait_ge(o_dma, 1 + 16 * (N + 1))
            with sp.Fori(2, NC) as c:
                wait_first(at_full, TT * (c - 1))
                wait_first(at_dma, 16 * c)
                load_heads(c)

            def load_slots(s, b):
                sp.dma_start(xs[:, b, :], slots_x[bass.ds(s * P, P), :]).then_inc(xs_dma[b], 16)

            def store_slots(s, b):
                wait_first(y_evac, SR + s + 1)
                sp.dma_start(slots_y[bass.ds(s * P, P), :], ys[:, b, :]).then_inc(ys_dma[b], 16)

            for b in range(SR):
                sp.wait_ge(sc_dma[b], 32 * (NKT // SR))
            for b in range(SR):
                load_slots(b, b)
            with sp.Fori(0, (NS - SR) // SR) as m:
                for b in range(SR):
                    wait_first(xt_full, m * SR + b + 1)
                    load_slots((m + 1) * SR + b, b)
                    store_slots(m * SR + b, b)
            for s in range((NS - SR) // SR * SR, NS):
                if s + SR < NS:
                    sp.wait_ge(xt_full, s + 1)
                    load_slots(s + SR, s % SR)
                store_slots(s, s % SR)

            with sp.Fori(0, NKT) as n:
                wait_first(sum2, SR + n + 1)
                sp.dma_start(out_t[:, bass.ds(n, 1), :], x2_all[:, bass.ds(n, 1), :]).then_inc(out_dma, 16)
            sp.wait_ge(out_dma, 16 * NKT)

        @block.scalar
        def _(act):
            for s, n in ((t_evac, 2), (p_ready, 3)):
                act.sem_inc(s, n)
            act.wait_ge(x_ready, 2)
            act.dma_start(wk_sb[:, :, :], Wk.rearrange("(k p) n -> p k n", p=P)).then_inc(wa_dma, 16)
            act.dma_start(wq_sb[:, :, :], Wq.rearrange("(k p) n -> p k n", p=P)).then_inc(wa_dma, 16)
            act.dma_start(wv_sb[:, :, :], Wv.rearrange("(k p) n -> p k n", p=P)).then_inc(wa_dma, 16)
            act.dma_start(bq_sb[:, :], bq).then_inc(wa_dma, 16)
            act.dma_start(bk_sb[:, :], bk).then_inc(wa_dma, 16)
            for t in range(TT):
                act.dma_start(bv_sb[:, t, :], bv.partition_broadcast(P)).then_inc(wa_dma, 16)
            act.wait_ge(consts, 1)

            def deviation(c):
                act.wait_ge(mv_ready, c + 1)
                act.activation(std[:, :], mv[:, :, 1], ACT.Sqrt, bias=eps_sb[:, 0:1]).then_inc(std_ready, 1)

            def evacuate_transposes(c):
                for t in range(TT):
                    act.wait_ge(t_full, c * TT + t + 1)
                    act.activation(xT[:, c, :, t * P:(t + 1) * P],
                                   bank[:, 6 + t % 2, :].rearrange("p (k s) -> p k s", k=KD),
                                   ACT.Copy).then_inc(t_evac, 1)

            def evacuate_projection(p):
                u = PROJ[p][1]
                act.wait_ge(proj_full, p + 1)
                bias = bk_sb[:, 0:1] if u == 0 else bq_sb[:, u - 1:u]
                act.activation(qf[:, u, :], bank[:, PROJ_BANK[p], :], ACT.Identity, bias=bias).then_inc(proj_evac, 1)
                act.wait_ge(proj_evac, p + 1)
                act.activation(parts[:, u, 0, :], qf[:, u, :], ACT.Copy).then_inc(hi_ready, 1)

            act.activation(table_warm[:, 0:1], eps_sb[:, :], ACT.Sqrt)
            deviation(0)
            evacuate_transposes(0)
            act.wait_ge(wa_dma, 16 * 9)
            deviation(1)
            for p in range(5):
                evacuate_projection(p)
            for c in range(1, NC):
                evacuate_transposes(c)
                if c < NC - 1:
                    deviation(c + 1)
                act.wait_ge(parts_stored, 16 * (4 + c))
                evacuate_projection(4 + c)
            for p in range(EARLY, len(PROJ)):
                if PROJ[p][1] == 1:
                    act.wait_ge(parts_stored, 16 * p)
                evacuate_projection(p)
                if p == EARLY + 3:
                    act.wait_ge(wo_dma, 16)
                    act.activation(wo_hi[:, :, :], wo_raw[:, :, :], ACT.Copy).then_inc(wo_split, 1)
                    act.activation(table_warm[:, 1:2], eps_sb[:, :], ACT.Exp)

            def copy_outputs(i):
                act.wait_ge(pv_done, PRING // REP + NKT * i)
                act.activation(o_acc[:, :], bank[:, 6, :], ACT.Copy).then_inc(o_ready, 1)

            with act.Fori(0, N) as i:
                for u in range(UNITS):
                    if u == 3:
                        copy_outputs(i)
                    act.wait_ge(s_full, UNITS * i + u + 1)
                    if u % REP == 0:
                        act.wait_ge(pv_done, NKT * i + u // REP + 1)
                    act.activation(probs[:, u % PRING, :], bank[:, ring_bank(("score", u)), :],
                                   ACT.Exp, scale=SCALE).then_inc(p_ready, 1)

            copy_outputs(N)

            def hi(dst, src):
                return act.activation(dst, src, ACT.Copy)

            def expert_hi(e):
                hi(we_hi[:, bass.ds(e, 1), :, :].squeeze(1), we_raw[:, bass.ds(e, 1), :, :].squeeze(1)).then_inc(we_split, 1)

            def attention_hi(n, t):
                act.wait_ge(at_full, n + 1)
                hi(atT_hi[:, t % 2, :, :], bank[:, 2 + t % 2, :].rearrange("p (k s) -> p k s", k=KD)).then_inc(at_hi, 1)

            def gate_evac(g, t):
                act.wait_ge(gt_full, g + 1)
                act.activation(xgT[:, t % 2, :, :], bank[:, t % 2, :].rearrange("p (k s) -> p k s", k=KD),
                               ACT.Copy).then_inc(gt_evac, 1)

            def logits_evac(k):
                act.wait_ge(lg_full, k + 1)
                act.activation(lgT[:, :], bank[0:E, 6, :], ACT.Copy).then_inc(lgT_ready, 1)

            def chunk(c, with_gate, last):
                for t in range(TT):
                    if not (last and t == TT - 1):
                        attention_hi(TT * c + t + 1, t + 1)
                    if with_gate:
                        gate_evac(TT * (c - 1) + t, t)
                        if t == 0 and not (isinstance(c, int) and c == 1):
                            logits_evac(c - 2)
                    if t == 1:
                        expert_hi(c)
                act.wait_ge(mv2_ready, c + 1)
                act.activation(std2[:, bass.ds(TT * c, TT)], mv2[:, bass.ds(TT * c, TT), 1],
                               ACT.Sqrt, bias=eps_sb[:, 0:1]).then_inc(std2_ready, 1)

            act.wait_ge(wc_dma, 16 * (3 + E))
            act.wait_ge(pv_done, PRING // REP + NKT * N)
            attention_hi(0, 0)
            chunk(0, False, False)
            chunk(1, True, False)
            with act.Fori(2, NC - 1) as c:
                chunk(c, True, False)
            chunk(NC - 1, True, True)
            for t in range(TT):
                gate_evac(TT * (NC - 1) + t, t)
                if t == 0:
                    logits_evac(NC - 2)
            logits_evac(NC - 1)
            act.wait_ge(gl_full, 1)
            def transposed_hi(q, b):
                act.wait_ge(xt_full, q + 1)
                hi(x2T_hi[:, b, :, :], bank[:, 5 + b, :].rearrange("p (k s) -> p k s", k=KD)).then_inc(xt_hi, 1)

            def output_evac(s, b):
                act.wait_ge(y_full, s + 1)
                act.wait_ge(ys_dma[b], 16 * (s // SR) + 16)
                act.activation(ys[:, b, :], bank[:, b, :], ACT.Copy).then_inc(y_evac, 1)

            act.wait_ge(gd_ready, 1)
            act.activation(g_exp[:, 1, :, :], g_exp[:, 0, :, :], ACT.Exp).then_inc(ge_ready, 1)
            for e in range(EA, E):
                expert_hi(e)
            with act.Fori(0, NKT // 2) as m:
                for b in range(2):
                    act.wait_ge(gT_full, 2 * m + b + 1)
                    act.activation(g_padT[:, b, :], bank[:, 7, b * P:(b + 1) * P], ACT.Copy).then_inc(gT_evac, 1)

            def slot_step(s, b):
                if not (isinstance(s, int) and s == NS - 1):
                    transposed_hi(s + 1, (b + 1) % 2)
                output_evac(s, b)

            transposed_hi(0, 0)
            with act.Fori(0, NS // SR) as m:
                for b in range(SR):
                    slot_step(m * SR + b, b)
            for s in range(NS // SR * SR, NS):
                slot_step(s, s % SR)

        @block.tensor
        def _(pe):
            pe.wait_ge(ident_ready, 1)
            pe.wait_ge(consts, 4)

            def transpose_chunk(c):
                for t in range(TT):
                    pe.wait_ge(xn_ready, c * TT + t + 1)
                    pe.wait_ge(t_evac, c * TT + t + 1)
                    for k in range(KD):
                        mm = pe.transpose(bank[:, 6 + t % 2, k * P:(k + 1) * P], xn[:, t, k * P:(k + 1) * P], ident[:, :])
                    mm.then_inc(t_full, 1)

            def projection_step(p, k):
                c, u = PROJ[p]
                before_p = [q for q in range(p) if PROJ_BANK[q] == PROJ_BANK[p]]
                if k == 0 and before_p:
                    pe.wait_ge(proj_evac, before_p[-1] + 1)
                w = wk_sb[:, k, :] if u == 0 else wq_sb[:, k, (u - 1) * P:u * P]
                mm = pe.matmul(bank[:, PROJ_BANK[p], :], w, xT[:, c, k, :], start=(k == 0), stop=(k == KD - 1))
                if k == KD - 1:
                    mm.then_inc(proj_full, 1)

            for c in range(NC):
                transpose_chunk(c)
                if c == 0:
                    pe.wait_ge(wa_dma, 16 * 9)
                pe.wait_ge(t_evac, 2 + TT * (c + 1))
                for k in range(KD):
                    projection_step(0 if c == 0 else 4 + c, k)
                if c > 0:
                    pe.wait_ge(v_evac, c)
                for t in range(TT):
                    for k in range(KD):
                        mm = pe.matmul(bank[:, 5, t * KVD:(t + 1) * KVD], xT[:, c, k, t * P:(t + 1) * P],
                                       wv_sb[:, k, :], start=(k == 0), stop=(k == KD - 1))
                mm.then_inc(v_full, 1)
                if c == 0:
                    for p in range(1, 5):
                        for k in range(KD):
                            projection_step(p, k)

            def max_unit(j, m):
                h, qt, half = m // (2 * TT), m // 2 % TT, m % 2
                pe.wait_ge(m_done, MUNITS * j + m + 1)
                qo = (j % SLOTS) * (REP * CH) + h * CH + qt * P
                for q in range(2):
                    mm = pe.matmul(bank[:, 2 + 2 * (m % 2) + q, :], q_flat[0:CROW, bass.ds(qo, P)],
                                   k_flat[0:CROW, bass.ds((j // NC) * T + (2 * half + q) * CH, CH)],
                                   start=True, stop=True)
                mm.then_inc(m_full, 1)

            def max_transpose(j):
                pe.wait_ge(maxq_ready, j + 1)
                pe.transpose(bank[0:REP * TT, B_MAX, 0:P], max_q[:, :], ident[:, :]).then_inc(mT_full, 1)

            def ring_bank_free(i, entry):
                r = RING.index(entry) - len(SBANKS)
                kind, u = RING[r]
                if r < 0:
                    pe.wait_ge(p_ready, UNITS * i + u - UNITS + len(SBANKS) + 1)
                elif kind == "score":
                    pe.wait_ge(p_ready, len(SBANKS) + UNITS * i + u + 1)
                elif kind == "outputs":
                    pe.wait_ge(onorm_ready, 2 + i)
                else:
                    pe.wait_ge(neg_ready, min(i, N - 2) + 3 if isinstance(i, int) else i + 3)

            def score_unit(i, u):
                kt, h = u // REP, u % REP
                ring_bank_free(i, ("score", u))
                qo = (i % SLOTS) * (REP * CH) + h * CH
                pe.matmul(bank[:, ring_bank(("score", u)), :], k_flat[0:SROW, bass.ds((i // NC) * T + kt * P, P)],
                          q_flat[0:SROW, bass.ds(qo, CH)], start=True, stop=True).then_inc(s_full, 1)

            def value_product(i, kt):
                pe.wait_ge(p_ready, len(SBANKS) + UNITS * i + REP * (kt + 1))
                for h in range(REP):
                    mm = pe.matmul(bank[32 * h:32 * h + 32, 6, :], v_cur[:, kt, :],
                                   probs[:, (REP * kt + h) % PRING, :],
                                   start=(kt == 0), stop=(kt == NKT - 1))
                mm.then_inc(pv_done, 1)

            def output_transpose(i):
                pe.wait_ge(o_ready, i + 1)
                if isinstance(i, int) and i == N:
                    pe.wait_ge(p_ready, len(SBANKS) + UNITS * N)
                else:
                    ring_bank_free(i, ("outputs", 0))
                for t in range(TT):
                    mm = pe.transpose(bank[:, B_OUT, t * P:(t + 1) * P], o_acc[:, t * P:(t + 1) * P], ident[:, :])
                mm.then_inc(oT_full, 1)

            steps = [(p, k) for p in range(EARLY, len(PROJ)) for k in range(KD)]
            ALONE = 14
            for p, k in steps[:ALONE]:
                projection_step(p, k)
            pe.wait_ge(proj_evac, EARLY)
            pe.wait_ge(v_evac, NC)
            pe.wait_ge(k0_dma, 16 * NTERM)
            pe.wait_ge(q_dma, 16 * NTERM)
            rest, units = len(steps) - ALONE, MUNITS + AHEAD
            for n in range(units):
                j, m = divmod(n, MUNITS)
                if n == MUNITS:
                    pe.wait_ge(q_dma, 16 * NTERM * 2)
                max_unit(j, m)
                if n == MUNITS + 1:
                    done = [q for q, _ in steps[:ALONE + n * rest // units] if PROJ_BANK[q] == B_MAX]
                    pe.wait_ge(proj_evac, done[-1] + 1)
                    max_transpose(0)
                if (n + 1) * rest // units > n * rest // units:
                    p, k = steps[ALONE + n * rest // units]
                    if n > MUNITS and k == 0 and PROJ_BANK[p] == B_MAX:
                        pe.wait_ge(neg_ready, 1 + 1)
                    projection_step(p, k)
            pe.wait_ge(proj_evac, len(PROJ))

            def attention_step(i, kt):
                j, m = maximum_of(i, kt)
                with_max = not isinstance(i, int) or j < N
                if kt == SPLIT and with_max:
                    pe.wait_ge(q_dma, 16 * NTERM * (j + 1))
                    pe.wait_ge(kr_dma, 16 * NTERM)
                    pe.wait_ge(ones_ready, 2)
                score_unit(i, REP * kt)
                score_unit(i, REP * kt + 1)
                if with_max:
                    max_unit(j, m)
                score_unit(i, REP * kt + 2)
                if kt >= 1:
                    if kt == 1:
                        pe.wait_ge(v_ready, i // NC + 1)
                        pe.wait_ge(o_ready, i + 1)
                    value_product(i, kt - 1)
                elif not (isinstance(i, int) and i == 0):
                    value_product(i - 1, NKT - 1)
                if kt == 2:
                    output_transpose(i)
                if kt == MAX_T and not (isinstance(i, int) and i == N - 1):
                    ring_bank_free(i, ("maxima", 0))
                    max_transpose(i + 1)
                if with_max:
                    max_unit(j, m + 1)
                score_unit(i, REP * kt + 3)

            def first_step(i):
                pe.wait_ge(shift_dma, 1 + 48 * (i + 1))
                attention_step(i, 0)

            def other_steps(i):
                for kt in range(1, NKT):
                    attention_step(i, kt)

            first_step(0)
            with pe.Fori(0, N - 2) as i:
                other_steps(i)
                first_step(i + 1)
            other_steps(N - 2)
            first_step(N - 1)
            other_steps(N - 1)
            value_product(N - 1, NKT - 1)
            output_transpose(N)

            def product(out_, lhs, rhs, first=True, last=True):
                terms = [(lhs[0], rhs[0]), (lhs[1], rhs[0]), (lhs[0], rhs[1])]
                for q, (a, w) in enumerate(terms):
                    for k in range(KD):
                        mm = pe.matmul(out_, a(k), w(k), start=(q == 0 and k == 0), stop=(q == 2 and k == KD - 1))
                return mm

            pe.wait_ge(m_done, 2 + MUNITS * N)
            pe.wait_ge(o_ready, N + 1)
            pe.wait_ge(p_ready, len(SBANKS) + UNITS * N)
            pe.wait_ge(wlo_ready, 1)
            def transpose_attention(n, t, half):
                pe.wait_ge(at_evac, n + 1)
                for k in range(KD):
                    mm = pe.transpose(bank[:, 2 + t % 2, k * P:(k + 1) * P], at[:, half, t, k * P:(k + 1) * P], ident[:, :])
                mm.then_inc(at_full, 1)

            def gate_transpose(g):
                pe.wait_ge(xg_ready, g + 1)
                pe.wait_ge(gt_evac, g + 1)
                for k in range(KD):
                    mm = pe.transpose(bank[:, g % 2, k * P:(k + 1) * P], xg[:, g % 2, k * P:(k + 1) * P], ident[:, :])
                mm.then_inc(gt_full, 1)

            def gate_logits(g):
                k, t = g // TT, g % TT
                if t == 0 and k > 0:
                    pe.wait_ge(lgT_ready, k)
                pe.wait_ge(gt_evac, 2 + g + 1)
                for d in range(KD):
                    mm = pe.matmul(bank[0:E, 6, t * P:(t + 1) * P], wg_sb[:, d, :], xgT[:, g % 2, d, :],
                                   start=(d == 0), stop=(d == KD - 1))
                if t == TT - 1:
                    mm.then_inc(lg_full, 1)

            def logits_back(k):
                pe.wait_ge(lgT_ready, k + 1)
                for t in range(TT):
                    n = k * TT + t
                    mm = pe.transpose(bank[:, 7, n * E:(n + 1) * E], lgT[:, t * P:(t + 1) * P], ident[0:E, 0:E])
                return mm

            def attention_chunk(c, half):
                for t in range(TT):
                    n, g = c * TT + t, (c - 1) * TT + t
                    if c < NC:
                        if t < TT - 1:
                            transpose_attention(n + 1, t + 1, half)
                        elif c < NC - 1:
                            pe.wait_ge(at_dma, 16 * (c + 2))
                            transpose_attention(n + 1, 0, 1 - half)
                        pe.wait_ge(at_evac, 2 + n + 1)
                        pe.wait_ge(x2_ready, n + 1)
                        product(bank[:, 4 + t % 2, :],
                                [lambda k: atT_hi[:, t % 2, k, :], lambda k: atT_lo[:, t % 2, k, :]],
                                [lambda k: wo_hi[:, k, :], lambda k: wo_lo[:, k, :]]).then_inc(wo_full, 1)
                    if c >= 1:
                        gate_transpose(g)
                        if g >= 1:
                            gate_logits(g - 1)
                        if t == 2 and c >= 2:
                            logits_back(c - 2)

            pe.wait_ge(onorm_ready, N + 2)
            pe.wait_ge(at_dma, 16)
            transpose_attention(0, 0, 1)
            pe.wait_ge(wc_dma, 16 * (3 + E))
            for c in range(NC + 1):
                attention_chunk(c, (c + 1) % 2)
            gate_logits(NKT - 1)
            logits_back(NC - 1).then_inc(gl_full, 1)

            def transpose_x(q, b, src):
                pe.wait_ge(xt_evac, q + 1)
                for k in range(KD):
                    mm = pe.transpose(bank[:, 5 + b, k * P:(k + 1) * P], src[:, k * P:(k + 1) * P], ident[:, :])
                mm.then_inc(xt_full, 1)

            def halves(b):
                return [lambda k: x2T_hi[:, b, k, :], lambda k: x2T_lo[:, b, k, :]]

            pe.wait_ge(chosen_ready, 1)
            pe.matmul(bank[:, 4, 256:256 + P], chosen[:, 0:NKT, :].rearrange("p n e -> p (n e)"), ones[:, :],
                      start=True, stop=True).then_inc(tot_full, 1)
            pe.wait_ge(tot_ready, 1)
            pe.matmul(bank[:, 4, 0:P + E], before[:, :], chosen[:, :, :].rearrange("p n e -> p (n e)"),
                      start=True, stop=False)
            pe.matmul(bank[:, 4, 0:P + E], totals[:, :], before_tile[:, :, :].rearrange("p n e -> p (n e)"),
                      start=False, stop=True).then_inc(rank_full, 1)

            with pe.Fori(0, NKT // 2) as m:
                for b in range(2):
                    n = 2 * m + b
                    pe.wait_ge(gw_ready, n + 1)
                    pe.transpose(bank[:, 7, b * P:(b + 1) * P], g_pad[:, b, :], ident[:, :]).then_inc(gT_full, 1)
                    pe.wait_ge(gT_evac, n + 1)
                    pe.wait_ge(bias_done, n + 1)
                    pe.matmul(bank[:, b, :], g_padT[:, b, :], be_sb[:, :], start=True, stop=True).then_inc(bias_full, 1)

            def transpose_slots(s, b):
                pe.wait_ge(xs_dma[b], 16 * (s // SR) + 16)
                transpose_x(s, b % 2, xs[:, b, :])

            def slot_step(s, b):
                expert = pe.value_load(expert_i[0:1, bass.ds(s, 1)], min_val=0, max_val=E - 1)
                if not (isinstance(s, int) and s == NS - 1):
                    transpose_slots(s + 1, (b + 1) % SR)
                pe.wait_ge(xt_evac, 2 + s + 1)
                pe.wait_ge(y_evac, s + 1)
                product(bank[:, b, :], halves(b % 2),
                        [lambda k: we_hi[:, bass.ds(expert, 1), k, :].squeeze(1),
                         lambda k: we_lo[:, bass.ds(expert, 1), k, :].squeeze(1)]).then_inc(y_full, 1)

            pe.wait_ge(elo_ready, E)
            pe.wait_ge(expert_ready, 1)
            pe.wait_ge(bias_done, 2 + NKT)
            transpose_slots(0, 0)
            with pe.Fori(0, NS // SR) as m:
                for b in range(SR):
                    slot_step(m * SR + b, b)
            for s in range(NS // SR * SR, NS):
                slot_step(s, s % SR)

        @block.vector
        def _(dve):
            for s, n in ((pv_done, PRING // REP), (m_done, 2), (neg_ready, 1),
                         (shift_dma, 1), (onorm_ready, 1), (o_dma, 1), (x2_ready, 2),
                         (at_evac, 2), (gt_evac, 2), (xt_evac, 2), (bias_done, 2), (y_evac, SR), (sum2, SR),
                         *((ys_dma[b], 16) for b in range(SR))):
                dve.sem_inc(s, n)
            dve.memset(eps_sb[:, :], EPS).then_inc(consts, 1)
            dve.memset(v_cur[:, :, DK:2 * DK], 1.0).then_inc(consts, 1)
            dve.memset(g_pad[:, :, :], 0.0).then_inc(consts, 1)
            dve.memset(be_sb[:, :], 0.0).then_inc(consts, 1)

            dve.wait_ge(ident_ready, 1)
            dve.reduce_sum(gates[:, 0, :], ident[:, :].rearrange("p (n e) -> p e n", e=E), AX.X).then_inc(consts, 1)
            dve.wait_ge(consts, 5)
            dve.tensor_copy(before_tile[:, :, :], gates[:, 0:1, :].to_broadcast([P, NKT + 1, E])).then_inc(eye_ready, 1)

            def chain(s, base):
                n = [0]

                def link(ins):
                    n[0] += 1
                    ins.then_inc(s, 1)
                    dve.wait_ge(s, base + n[0])
                    dve.sem_inc(dve_passed, 1)
                return link

            STEPS_N = TT * 2 + 1

            def normalise_chunk(c):
                link = chain(step_n, STEPS_N * c)
                for t in range(TT):
                    dve.wait_ge(x_ready, t + 1 if c == 0 else TT + c)
                    link(dve.bn_stats(stats[:, t, :], x_all[:, bass.ds(c * TT + t, 1), :].squeeze(1)))
                for t in range(TT):
                    link(dve.bn_aggr(mv[:, t, :], stats[:, t, :]))
                dve.sem_inc(mv_ready, 1)
                dve.wait_ge(std_ready, c + 1)
                link(dve.reciprocal(rstd[:, :], std[:, :]))
                if c > 0:
                    dve.wait_ge(t_full, TT * c)
                for t in range(TT):
                    dve.tensor_scalar(xn[:, t, :], x_all[:, bass.ds(c * TT + t, 1), :].squeeze(1), mv[:, t, 0:1],
                                      rstd[:, t:t + 1], ALU.subtract, ALU.mult).then_inc(xn_ready, 1)

            def evacuate_values(c):
                dve.wait_ge(v_full, c + 1)
                dve.tensor_tensor(v_all[:, c * TT:(c + 1) * TT, :], bank[:, 5, :].rearrange("p (t n) -> p t n", t=TT),
                                  bv_sb[:, :, :], ALU.add).then_inc(v_evac, 1)

            normalise_chunk(0)
            for c in range(1, NC):
                normalise_chunk(c)
                evacuate_values(c - 1)
            evacuate_values(NC - 1)

            def reduce_unit(j, m):
                dve.wait_ge(m_full, MUNITS * j + m + 1)
                dve.reduce_max(max_kc[:, m:m + 1], bank[:, 2 + 2 * (m % 2):4 + 2 * (m % 2), :].rearrange("p a s -> p (a s)"),
                               AX.X).then_inc(m_done, 1)

            def combine_max(j):
                dve.wait_ge(m_done, 2 + MUNITS * (j + 1))
                dve.reduce_max(max_q[:, :], max_kc[:, :].rearrange("p (r c) -> p r c", c=2),
                               AX.X).then_inc(maxq_ready, 1)

            def make_shift(j, part):
                base = 3 * j
                if part == 0:
                    dve.wait_ge(mT_full, j + 1)
                    dve.wait_ge(shift_dma, 1 + 48 * j)
                    dve.tensor_scalar(negmax[:, :], bank[0:REP * TT, B_MAX, 0:P], -1.0, None,
                                      ALU.mult).then_inc(neg_ready, 1)
                elif part == 1:
                    dve.wait_ge(neg_ready, 1 + j + 1)
                    dve.tensor_copy(shift[:, 0, :], negmax[:, :]).then_inc(step_m, 1)
                elif part == 2:
                    dve.wait_ge(step_m, base + 1)
                    dve.tensor_tensor(negmax[:, :], negmax[:, :], shift[:, 0, :], ALU.subtract).then_inc(step_m, 1)
                elif part == 3:
                    dve.wait_ge(step_m, base + 2)
                    dve.tensor_copy(shift[:, 1, :], negmax[:, :]).then_inc(step_m, 1)
                else:
                    dve.wait_ge(step_m, base + 3)
                    dve.tensor_tensor(shift[:, 2, :], negmax[:, :], shift[:, 1, :],
                                      ALU.subtract).then_inc(shift_ready, 1)

            def normalise(i):
                dve.wait_ge(oT_full, i + 1)
                dve.wait_ge(o_dma, 1 + 16 * i)
                o = bank[:, B_OUT, :].rearrange("p (t h f) -> p t h f", t=TT, h=REP)
                dve.reciprocal(o_rec[:, :, :, :], o[:, :, :, DK:DK + 1]).then_inc(rec_ready, 1)
                dve.wait_ge(rec_ready, i + 1)
                dve.tensor_tensor(o_norm[:, :, :, :], o[:, :, :, 0:DK], o_rec[:, :, :, :].to_broadcast([P, TT, REP, DK]),
                                  ALU.mult).then_inc(onorm_ready, 1)

            for m in range(MUNITS):
                reduce_unit(0, m)
            combine_max(0)
            dve.wait_ge(maxq_ready, 1)
            for m in range(AHEAD):
                reduce_unit(1, m)
                if 2 <= m < 7:
                    make_shift(0, m - 2)

            def round_(i):
                last = isinstance(i, int) and i == N - 1
                for kt in range(NKT):
                    for half in range(2):
                        j, m = maximum_of(i, kt)
                        if not isinstance(i, int) or j < N:
                            reduce_unit(j, m + half)
                        if kt == 2 and half == 0:
                            normalise(i)
                        part = 2 * (kt - MAX_T) + half
                        if 0 <= part < 5 and not last:
                            make_shift(i + 1, part)
                    if kt == SPLIT and last:
                        dve.wait_ge(wo_split, 1)
                        dve.tensor_tensor(wo_lo[:, :, :], wo_raw[:, :, :], wo_hi[:, :, :],
                                          ALU.subtract).then_inc(wlo_ready, 1)
                    if kt == SPLIT - 1 and not last:
                        combine_max(i + 1)
                        dve.wait_ge(maxq_ready, i + 2)

            with dve.Fori(0, N - 2) as i:
                round_(i)
            round_(N - 2)
            round_(N - 1)
            normalise(N)

            def expert_lo(e):
                dve.wait_ge(we_split, e + 1)
                dve.tensor_tensor(we_lo[:, bass.ds(e, 1), :, :].squeeze(1), we_raw[:, bass.ds(e, 1), :, :].squeeze(1),
                                  we_hi[:, bass.ds(e, 1), :, :].squeeze(1), ALU.subtract).then_inc(elo_ready, 1)

            def attention_lo(n, t):
                dve.wait_ge(at_hi, n + 1)
                dve.tensor_tensor(atT_lo[:, t % 2, :, :], bank[:, 2 + t % 2, :].rearrange("p (k s) -> p k s", k=KD),
                                  atT_hi[:, t % 2, :, :], ALU.subtract).then_inc(at_evac, 1)

            STEPS_C = TT * 2 + 2

            def gate_tile(g, t):
                dve.wait_ge(gt_evac, g + 1)
                dve.sem_inc(dve_passed, 1)
                dve.tensor_scalar(xg[:, t % 2, :], x2_all[:, bass.ds(g, 1), :].squeeze(1),
                                  mv2[:, bass.ds(g, 1), 0], rstd2[:, bass.ds(g, 1)],
                                  ALU.subtract, ALU.mult).then_inc(xg_ready, 1)

            def deviations(c):
                dve.wait_ge(std2_ready, c)
                dve.reciprocal(rstd2[:, bass.ds(TT * (c - 1), TT)], std2[:, bass.ds(TT * (c - 1), TT)]).then_inc(step_c, 1)
                dve.wait_ge(step_c, STEPS_C * c)
                dve.sem_inc(dve_passed, 1)

            def attention_chunk(c, with_gate, last):
                base = STEPS_C * c

                def passed(step):
                    dve.wait_ge(step_c, base + step)
                    dve.sem_inc(dve_passed, 1)

                for t in range(TT):
                    if not (last and t == TT - 1):
                        attention_lo(c * TT + t + 1, t + 1)
                    if with_gate:
                        if t == 0:
                            deviations(c)
                        gate_tile(TT * (c - 1) + t, t)
                    tile = x2_all[:, bass.ds(c * TT + t, 1), :].squeeze(1)
                    dve.wait_ge(wo_full, TT * c + t + 1)
                    dve.wait_ge(xb_ready, TT * c + t + 1)
                    dve.tensor_tensor(tile, bank[:, 4 + t % 2, :], tile, ALU.add).then_inc(x2_ready, 1)
                    if t > 0:
                        passed(2 * t - 1)
                        dve.bn_aggr(mv[:, t - 1, :], stats[:, t - 1, :]).then_inc(step_c, 1)
                    dve.wait_ge(x2_ready, 2 + TT * c + t + 1)
                    dve.sem_inc(dve_passed, 1)
                    dve.bn_stats(stats[:, t, :], tile).then_inc(step_c, 1)
                    if t == 2:
                        expert_lo(c)
                passed(2 * TT - 1)
                dve.bn_aggr(mv[:, TT - 1, :], stats[:, TT - 1, :]).then_inc(step_c, 1)
                passed(2 * TT)
                dve.tensor_copy(mv2[:, bass.ds(c * TT, TT), :], mv[:, :, :]).then_inc(step_c, 1)
                passed(2 * TT + 1)
                dve.sem_inc(mv2_ready, 1)

            attention_lo(0, 0)
            attention_chunk(0, False, False)
            with dve.Fori(1, NC - 1) as c:
                attention_chunk(c, True, False)
            attention_chunk(NC - 1, True, True)
            deviations(NC)
            for t in range(TT):
                gate_tile(TT * (NC - 1) + t, t)

            def normalise_tile(n, b):
                dve.tensor_scalar(xn2[:, b, :], x2_all[:, bass.ds(n, 1), :].squeeze(1),
                                  mv2[:, bass.ds(n, 1), 0], rstd2[:, bass.ds(n, 1)],
                                  ALU.subtract, ALU.mult).then_inc(xn2_ready, 1)

            def transposed_lo(q, b):
                dve.wait_ge(xt_hi, q + 1)
                dve.tensor_tensor(x2T_lo[:, b, :, :], bank[:, 5 + b, :].rearrange("p (k s) -> p k s", k=KD),
                                  x2T_hi[:, b, :, :], ALU.subtract).then_inc(xt_evac, 1)

            for n in range(SR):
                normalise_tile(n, n)

            link = chain(step_g, 0)
            tok = [P, NKT, E]
            dve.wait_ge(gl_full, 1)
            link(dve.memset(chosen[:, NKT:NKT + 1, :], 0.0))
            link(dve.tensor_copy(logits[:, :, :], bank[:, 7, 0:NKT * E].rearrange("p (n e) -> p n e", e=E)))

            def choose(src, a, mask):
                link(dve.reduce_max(top[:, 2 * a, :, :].squeeze(2), src[:, :, :], AX.X))
                link(dve.tensor_tensor(pick[:, :, :], src[:, :, :], top[:, 2 * a, :, :].to_broadcast(tok), ALU.is_equal))
                link(dve.tensor_tensor(pick[:, :, :], pick[:, :, :], rev[:, :, :], ALU.mult))
                link(dve.reduce_max(top[:, 2 * a + 1, :, :].squeeze(2), pick[:, :, :], AX.X))
                link(dve.tensor_tensor(mask[:, :, :], rev[:, :, :], top[:, 2 * a + 1, :, :].to_broadcast(tok),
                                       ALU.is_equal))

            choose(logits, 0, first)
            link(dve.scalar_tensor_tensor(logits2[:, :, :], first[:, :, :], -3e38, logits[:, :, :], ALU.mult, ALU.add))
            choose(logits2, 1, second)
            dve.tensor_tensor(chosen[:, 0:NKT, :], first[:, :, :], second[:, :, :], ALU.add).then_inc(chosen_ready, 1)
            dve.tensor_tensor(g_exp[:, 0, :, :], top[:, 2, :, :], top[:, 0, :, :], ALU.subtract).then_inc(gd_ready, 1)
            dve.wait_ge(tot_full, 1)
            dve.tensor_copy(totals[:, :], bank[:, 4, 256:256 + P]).then_inc(tot_ready, 1)

            dve.wait_ge(rank_full, 1)
            link(dve.tensor_copy(counts[:, :], bank[:, 4, P:P + E]))
            link(dve.tensor_tensor(grid[:, :, :], counts[:, :].unsqueeze(2).to_broadcast([P, E, NKT]), steps128[:, :, :],
                                   ALU.is_gt))
            link(dve.reduce_sum(tiles_of[:, 0, :], grid[:, :, :], AX.X))
            link(dve.tensor_tensor(grid8[:, :, :], tiles_of[:, 0:1, :].to_broadcast([P, E, E]), upto[:, :, :], ALU.mult))
            link(dve.reduce_sum(tiles_of[:, 1, :], grid8[:, :, :], AX.X))
            link(dve.tensor_tensor(tiles_of[:, 2, :], tiles_of[:, 1, :], tiles_of[:, 0, :], ALU.subtract))
            link(dve.tensor_scalar(tiles_of[:, 2, :], tiles_of[:, 2, :], float(P), None, ALU.mult))
            link(dve.tensor_tensor(pick[:, :, :], bank[:, 4, 0:P].rearrange("p (n e) -> p n e", e=E),
                                   tiles_of[:, 2:3, :].to_broadcast(tok), ALU.add))
            link(dve.tensor_tensor(logits[:, :, :], pick[:, :, :], first[:, :, :], ALU.mult))
            link(dve.tensor_tensor(logits2[:, :, :], pick[:, :, :], second[:, :, :], ALU.mult))
            link(dve.reduce_sum(slot_f[:, 0, :], logits[:, :, :], AX.X))
            link(dve.reduce_sum(slot_f[:, 1, :], logits2[:, :, :], AX.X))
            dve.tensor_copy(slot_i[:, :, :], slot_f[:, :, :]).then_inc(slots_ready, 1)

            link(dve.tensor_tensor(expert_cmp[:, :, :], tiles_of[0:1, 1:2, :].to_broadcast([1, NS, E]),
                                   slot_no[:, :, :], ALU.is_le))
            link(dve.reduce_sum(expert_f[:, :], expert_cmp[:, :, :], AX.X))
            link(dve.tensor_scalar(expert_f[:, :], expert_f[:, :], float(E - 1), None, ALU.min))
            dve.tensor_copy(expert_i[:, :], expert_f[:, :]).then_inc(expert_ready, 1)

            dve.wait_ge(ge_ready, 1)
            link(dve.tensor_scalar(g_exp[:, 2, :, :], g_exp[:, 1, :, :], 1.0, None, ALU.add))
            link(dve.reciprocal(g_w[:, 0, :, :], g_exp[:, 2, :, :]))
            link(dve.tensor_tensor(g_w[:, 1, :, :], g_exp[:, 1, :, :], g_w[:, 0, :, :], ALU.mult))

            link(dve.tensor_tensor(first[:, :, :], first[:, :, :], g_w[:, 0, :, :].to_broadcast(tok), ALU.mult))
            link(dve.tensor_tensor(second[:, :, :], second[:, :, :], g_w[:, 1, :, :].to_broadcast(tok), ALU.mult))
            link(dve.tensor_tensor(gates[:, :, :], first[:, :, :], second[:, :, :], ALU.add))

            def gate_columns(n, b):
                dve.tensor_copy(g_pad[:, b, 0:E], gates[:, bass.ds(n, 1), :].squeeze(1)).then_inc(gw_ready, 1)

            def add_bias(n, b):
                tile = x2_all[:, bass.ds(n, 1), :].squeeze(1)
                dve.wait_ge(bias_full, n + 1)
                dve.tensor_tensor(tile, bank[:, b, :], tile, ALU.add).then_inc(bias_done, 1)

            gate_columns(0, 0)
            gate_columns(1, 1)
            for n in range(NKT):
                if n + 2 < NKT and n + 2 >= SR:
                    dve.wait_ge(sc_dma[(n + 2) % SR], 32 * ((n + 2) // SR))
                    dve.sem_inc(dve_passed, 1)
                    normalise_tile(n + 2, (n + 2) % SR)
                add_bias(n, n % 2)
                if n + 2 < NKT:
                    gate_columns(n + 2, n % 2)
                if n % 4 == 3:
                    expert_lo(EA + n // 4)

            with dve.Fori(0, (NS - 1) // 2) as m:
                for b in range(2):
                    transposed_lo(2 * m + b, b)
            transposed_lo(NS - 1, 0)

            for n in range(NKT):
                dve.wait_ge(yt_dma[n % SR], 32 * (n // SR + 1))
                dve.wait_ge(bias_done, 2 + n + 1)
                dve.scalar_tensor_tensor(x2_all[:, n, :], xs[:, n % SR, :], g_w[:, 0, n, :], x2_all[:, n, :],
                                         ALU.mult, ALU.add).then_inc(sum1, 1)
                dve.wait_ge(sum1, n + 1)
                dve.scalar_tensor_tensor(x2_all[:, n, :], ys[:, n % SR, :], g_w[:, 1, n, :], x2_all[:, n, :],
                                         ALU.mult, ALU.add).then_inc(sum2, 1)


_INS = ["L0_attn_x", "L0_attn_Wq", "L0_attn_bq", "L0_attn_Wk", "L0_attn_bk", "L0_attn_Wv", "L0_attn_bv",
        "L0_attn_Wo", "L0_attn_bo", "L0_ffn_gate_w", "L0_ffn_expert_w", "L0_ffn_expert_b"]


def kernel(**inputs):
    import numpy as np
    import concourse.bacc as bacc
    from concourse.bass_utils import run_bass_kernel_spmd

    nc = bacc.Bacc("TRN2", target_bir_lowering=False, num_devices=1)
    arrays, args = {}, []
    for name in _INS:
        a = np.asarray(inputs[name])
        if name == "L0_ffn_expert_w":
            a = a.transpose(0, 2, 1)
        if name == "L0_ffn_gate_w":
            a = a.T
        if name in ("L0_attn_bq", "L0_attn_bk"):
            a = a.reshape(-1, P).T
        a = np.ascontiguousarray(a)
        arrays[f"in_{name}"] = a
        args.append(nc.dram_tensor(f"in_{name}", a.shape, mybir.dt.from_np(a.dtype), kind="ExternalInput").ap())
    out = nc.dram_tensor("out_y", arrays["in_L0_attn_x"].shape, F32, kind="ExternalOutput").ap()
    preln_attention_moe(nc, *args, out)
    r = run_bass_kernel_spmd(nc, [arrays], core_ids=[0])
    return r.results[0]["out_y"]
```
